# Optimizing a Trainium2 kernel written in Bass

```python
import numpy as np
import jax
import jax.numpy as jnp

def _softmax(x, axis=-1):
    return jax.nn.softmax(x, axis=axis)
def _gelu(x):
    return jax.nn.gelu(x, approximate=True)
def _silu(x):
    return jax.nn.silu(x)
def _sigmoid(x):
    return jax.nn.sigmoid(x)
def _layernorm(x, axis=-1, eps=1e-5):
    m = jnp.mean(x, axis=axis, keepdims=True)
    v = jnp.var(x, axis=axis, keepdims=True)
    return (x - m) / jnp.sqrt(v + eps)
def _scatter_add(tgt, idx, src, axis=0):
    return tgt.at[idx].add(src)
def _segment_sum(src, seg, n):
    return jax.ops.segment_sum(src, seg, n)

kernel_name = 'mk_conv_preact_d2_conv_nchw192_b97d4a'

def setup_inputs(seed: int = 0):
    np.random.seed(seed)
    _w = jnp.asarray
    def _rec_inputs():
        import jax
        import jax.numpy as jnp
        _gk = jax.random.key(seed)
        x = -0.0002221 + 1 * jax.random.normal(jax.random.fold_in(_gk, 1), (8, 192, 128, 128), jnp.float32)
        return x
    x = _rec_inputs()
    def _L0_conv_setup():
        import jax, jax.numpy as jnp
        import numpy as np
        from jax import lax
        DIM, HID, PS = (192, 510, 2)

        def _dffn(x, w_in, w_dw, fft_w, w_out):
            B, _, H, W = x.shape
            hid = w_in.shape[0]
            h = jnp.einsum('bchw,oc->bohw', x, w_in[:, :, 0, 0])
            hp = h.reshape(B, hid, H // PS, PS, W // PS, PS).transpose(0, 1, 2, 4, 3, 5)
            fr = jnp.fft.rfft2(hp) * fft_w
            hp = jnp.fft.irfft2(fr, s=(PS, PS))
            h = hp.transpose(0, 1, 2, 4, 3, 5).reshape(B, hid, H, W)
            d = lax.conv_general_dilated(h, w_dw, window_strides=(1, 1), padding=((1, 1), (1, 1)), dimension_numbers=('NCHW', 'OIHW', 'NCHW'), feature_group_count=hid)
            x1, x2 = (d[:, :hid], d[:, hid:])
            g = jax.nn.gelu(x1, approximate=False) * x2
            return jnp.einsum('bchw,oc->bohw', g, w_out[:, :, 0, 0])
        key = jax.random.key(seed)
        k1, k2, k3, k4, k5 = jax.random.split(key, 5)
        return {'x': jax.random.normal(k1, (8, DIM, 128, 128), dtype=jnp.float32), 'w_in': jax.random.normal(k2, (HID, DIM, 1, 1), dtype=jnp.float32) * 0.05, 'w_dw': jax.random.normal(k3, (2 * HID, 1, 3, 3), dtype=jnp.float32) * 0.1, 'fft_w': jnp.ones((HID, 1, 1, PS, PS // 2 + 1), dtype=jnp.float32) + 0.1 * jax.random.normal(k4, (HID, 1, 1, PS, PS // 2 + 1), dtype=jnp.float32), 'w_out': jax.random.normal(k5, (DIM, HID, 1, 1), dtype=jnp.float32) * 0.05}
    _L0_conv_all = _L0_conv_setup()
    _L0_conv_in = {k: v for k, v in _L0_conv_all.items() if k in ('w_in', 'w_dw', 'fft_w', 'w_out', )}
    del _L0_conv_all

    def _L1_conv_setup():
        import jax, jax.numpy as jnp
        import numpy as np
        import math
        C64 = jnp.complex64

        def _fftconv_full(a, kern):
            L = a.shape[-1] + kern.shape[0] - 1
            A = jnp.fft.fft(a, n=L, axis=-1)
            K = jnp.fft.fft(kern.astype(a.dtype), n=L)
            return jnp.fft.ifft(A * K, axis=-1)

        def _centered_ifft(f):
            N = f.shape[-1]
            shft = (np.arange(N) + int(np.fix(N / 2))) % N
            inv = np.argsort(shft)
            g = jnp.fft.ifft(f[..., shft], axis=-1) * math.sqrt(N)
            return g[..., inv].astype(f.dtype)

        def _sincinterp(f):
            N = f.shape[-1]
            y = jnp.zeros(f.shape[:-1] + (2 * N - 1,), f.dtype).at[..., ::2].set(f)
            kern = jnp.asarray(np.sinc(np.arange(-(2 * N - 3), 2 * N - 2) / 2.0).astype(np.complex64))
            return _fftconv_full(y, kern)[..., 2 * N - 3:4 * N - 4]

        def _frft_chirp(f, a):
            N = f.shape[-1]
            alpha = a * math.pi / 2
            tana2, sina = (math.tan(alpha / 2), math.sin(alpha))
            fi = _sincinterp(f)
            pad = jnp.zeros(f.shape[:-1] + (N - 1,), f.dtype)
            fp = jnp.concatenate([pad, fi, pad], axis=-1)
            n = np.arange(-2 * N + 2, 2 * N - 1).astype(np.float64)
            chrp = jnp.asarray(np.exp(-1j * math.pi / N * tana2 / 4 * n ** 2).astype(np.complex64))
            fp = chrp * fp
            c = math.pi / N / sina / 4
            m = np.arange(-(4 * N - 4), 4 * N - 3).astype(np.float64)
            kern = jnp.asarray(np.exp(1j * c * m ** 2).astype(np.complex64))
            ret = _fftconv_full(fp, kern)[..., 4 * N - 4:8 * N - 7] * math.sqrt(c / math.pi)
            ret = chrp * ret
            phase = np.complex64(np.exp(-1j * (1 - a) * math.pi / 4))
            return phase * ret[..., N - 1:3 * N - 2:2]

        def _frft_last(f, a):
            if a < 0.5:
                f = _centered_ifft(f)
                a = a + 1.0
            return _frft_chirp(f, a)

        def _frft2d(x, a):
            t = _frft_last(x, a)
            return jnp.swapaxes(_frft_last(jnp.swapaxes(t, -1, -2), a), -1, -2)

        def _c1x1(x, w, b=None):
            y = jnp.einsum('nchw,oc->nohw', x, w)
            return y if b is None else y + b[None, :, None, None]

        def _c3x3(x, w, b):
            y = jax.lax.conv_general_dilated(x, w, (1, 1), 'SAME', dimension_numbers=('NCHW', 'OIHW', 'NCHW'))
            return y + b[None, :, None, None]

        def _forward(x, conv1_w, mag_s_w, mag_s_b, mag_f_w, mag_f_b, mag_w, mag_b, pha_w, pha_b, conv_0_w, conv_0_b, conv_1_w, conv_1_b, conv2_w):
            angle = 0.5
            alpha = math.cos(angle * math.pi / 2)
            N, C, H, W = x.shape
            H1, W1 = (int(H * alpha), int(W * alpha))
            x1 = _c1x1(x, conv1_w)
            C1, C0 = (C // 4, C // 4 // 3)
            x_0, x_05, x_1 = (x1[:, :C0], x1[:, C0:C1 - C0], x1[:, C1 - C0:C1])
            h0, w0 = ((H - H1) // 2, (W - W1) // 2)
            mask1 = jnp.zeros((H, W), jnp.float32).at[h0:h0 + H1, w0:w0 + W1].set(1.0)
            mask2 = 1.0 - mask1
            Fre = _frft2d(x_05.astype(C64), angle)
            mag, pha = (jnp.abs(Fre), jnp.angle(Fre))
            mag_out = _c1x1(_c3x3(mag * mask1, mag_s_w, mag_s_b) * mask1 + _c1x1(mag * mask2, mag_f_w, mag_f_b) * mask2, mag_w, mag_b)
            pha_out = _c1x1(pha, pha_w, pha_b)
            Fre_out = jax.lax.complex(mag_out * jnp.cos(pha_out), mag_out * jnp.sin(pha_out))
            ifrft = jnp.abs(_frft2d(Fre_out, -angle))
            fre = jnp.fft.rfft2(x_1)
            fm, fp = (jnp.abs(fre), jnp.angle(fre))
            mo = _c1x1(fm, conv_1_w, conv_1_b)
            po = _c1x1(fp, conv_1_w, conv_1_b)
            x_1o = jnp.fft.irfft2(jax.lax.complex(mo * jnp.cos(po), mo * jnp.sin(po)), s=(H, W))
            x_0o = _c1x1(x_0, conv_0_w, conv_0_b)
            return _c1x1(jnp.concatenate([x_0o, ifrft, x_1o], axis=1), conv2_w)
        key = jax.random.key(seed)
        ks = jax.random.split(key, 16)
        N, C, H, W, Co = (4, 192, 128, 128, 192)
        C1, C0 = (C // 4, C // 4 // 3)
        Cm = C1 - 2 * C0
        s = 0.05
        r = lambda k, sh: jax.random.normal(k, sh, jnp.float32)
        return {'x': r(ks[0], (N, C, H, W)), 'conv1_w': r(ks[1], (C1, C)) * s, 'mag_s_w': r(ks[2], (Cm, Cm, 3, 3)) * s, 'mag_s_b': r(ks[3], (Cm,)) * s, 'mag_f_w': r(ks[4], (Cm, Cm)) * s, 'mag_f_b': r(ks[5], (Cm,)) * s, 'mag_w': r(ks[6], (Cm, Cm)) * s, 'mag_b': r(ks[7], (Cm,)) * s, 'pha_w': r(ks[8], (Cm, Cm)) * s, 'pha_b': r(ks[9], (Cm,)) * s, 'conv_0_w': r(ks[10], (C0, C0)) * s, 'conv_0_b': r(ks[11], (C0,)) * s, 'conv_1_w': r(ks[12], (C0, C0)) * s, 'conv_1_b': r(ks[13], (C0,)) * s, 'conv2_w': r(ks[14], (Co, C1)) * s}
    _L1_conv_all = _L1_conv_setup()
    _L1_conv_in = {k: v for k, v in _L1_conv_all.items() if k in ('conv1_w', 'mag_s_w', 'mag_s_b', 'mag_f_w', 'mag_f_b', 'mag_w', 'mag_b', 'pha_w', 'pha_b', 'conv_0_w', 'conv_0_b', 'conv_1_w', 'conv_1_b', 'conv2_w', )}
    del _L1_conv_all

    return {
        "x": x,
        "L0_conv_w_in": _L0_conv_in["w_in"],
        "L0_conv_w_dw": _L0_conv_in["w_dw"],
        "L0_conv_fft_w": _L0_conv_in["fft_w"],
        "L0_conv_w_out": _L0_conv_in["w_out"],
        "L1_conv_conv1_w": _L1_conv_in["conv1_w"],
        "L1_conv_mag_s_w": _L1_conv_in["mag_s_w"],
        "L1_conv_mag_s_b": _L1_conv_in["mag_s_b"],
        "L1_conv_mag_f_w": _L1_conv_in["mag_f_w"],
        "L1_conv_mag_f_b": _L1_conv_in["mag_f_b"],
        "L1_conv_mag_w": _L1_conv_in["mag_w"],
        "L1_conv_mag_b": _L1_conv_in["mag_b"],
        "L1_conv_pha_w": _L1_conv_in["pha_w"],
        "L1_conv_pha_b": _L1_conv_in["pha_b"],
        "L1_conv_conv_0_w": _L1_conv_in["conv_0_w"],
        "L1_conv_conv_0_b": _L1_conv_in["conv_0_b"],
        "L1_conv_conv_1_w": _L1_conv_in["conv_1_w"],
        "L1_conv_conv_1_b": _L1_conv_in["conv_1_b"],
        "L1_conv_conv2_w": _L1_conv_in["conv2_w"],
    }

def reference(x, L0_conv_w_in, L0_conv_w_dw, L0_conv_fft_w, L0_conv_w_out, L1_conv_conv1_w, L1_conv_mag_s_w, L1_conv_mag_s_b, L1_conv_mag_f_w, L1_conv_mag_f_b, L1_conv_mag_w, L1_conv_mag_b, L1_conv_pha_w, L1_conv_pha_b, L1_conv_conv_0_w, L1_conv_conv_0_b, L1_conv_conv_1_w, L1_conv_conv_1_b, L1_conv_conv2_w):
    import jax
    import jax.numpy as jnp
    def _L0_conv_ref(x, w_in, w_dw, fft_w, w_out):
        import jax, jax.numpy as jnp
        import numpy as np
        from jax import lax
        DIM, HID, PS = (192, 510, 2)

        def _dffn(x, w_in, w_dw, fft_w, w_out):
            B, _, H, W = x.shape
            hid = w_in.shape[0]
            h = jnp.einsum('bchw,oc->bohw', x, w_in[:, :, 0, 0])
            hp = h.reshape(B, hid, H // PS, PS, W // PS, PS).transpose(0, 1, 2, 4, 3, 5)
            fr = jnp.fft.rfft2(hp) * fft_w
            hp = jnp.fft.irfft2(fr, s=(PS, PS))
            h = hp.transpose(0, 1, 2, 4, 3, 5).reshape(B, hid, H, W)
            d = lax.conv_general_dilated(h, w_dw, window_strides=(1, 1), padding=((1, 1), (1, 1)), dimension_numbers=('NCHW', 'OIHW', 'NCHW'), feature_group_count=hid)
            x1, x2 = (d[:, :hid], d[:, hid:])
            g = jax.nn.gelu(x1, approximate=False) * x2
            return jnp.einsum('bchw,oc->bohw', g, w_out[:, :, 0, 0])
        return _dffn(x, w_in, w_dw, fft_w, w_out)

    def _L1_conv_ref(x, conv1_w, mag_s_w, mag_s_b, mag_f_w, mag_f_b, mag_w, mag_b, pha_w, pha_b, conv_0_w, conv_0_b, conv_1_w, conv_1_b, conv2_w):
        import jax, jax.numpy as jnp
        import numpy as np
        import math
        C64 = jnp.complex64

        def _fftconv_full(a, kern):
            L = a.shape[-1] + kern.shape[0] - 1
            A = jnp.fft.fft(a, n=L, axis=-1)
            K = jnp.fft.fft(kern.astype(a.dtype), n=L)
            return jnp.fft.ifft(A * K, axis=-1)

        def _centered_ifft(f):
            N = f.shape[-1]
            shft = (np.arange(N) + int(np.fix(N / 2))) % N
            inv = np.argsort(shft)
            g = jnp.fft.ifft(f[..., shft], axis=-1) * math.sqrt(N)
            return g[..., inv].astype(f.dtype)

        def _sincinterp(f):
            N = f.shape[-1]
            y = jnp.zeros(f.shape[:-1] + (2 * N - 1,), f.dtype).at[..., ::2].set(f)
            kern = jnp.asarray(np.sinc(np.arange(-(2 * N - 3), 2 * N - 2) / 2.0).astype(np.complex64))
            return _fftconv_full(y, kern)[..., 2 * N - 3:4 * N - 4]

        def _frft_chirp(f, a):
            N = f.shape[-1]
            alpha = a * math.pi / 2
            tana2, sina = (math.tan(alpha / 2), math.sin(alpha))
            fi = _sincinterp(f)
            pad = jnp.zeros(f.shape[:-1] + (N - 1,), f.dtype)
            fp = jnp.concatenate([pad, fi, pad], axis=-1)
            n = np.arange(-2 * N + 2, 2 * N - 1).astype(np.float64)
            chrp = jnp.asarray(np.exp(-1j * math.pi / N * tana2 / 4 * n ** 2).astype(np.complex64))
            fp = chrp * fp
            c = math.pi / N / sina / 4
            m = np.arange(-(4 * N - 4), 4 * N - 3).astype(np.float64)
            kern = jnp.asarray(np.exp(1j * c * m ** 2).astype(np.complex64))
            ret = _fftconv_full(fp, kern)[..., 4 * N - 4:8 * N - 7] * math.sqrt(c / math.pi)
            ret = chrp * ret
            phase = np.complex64(np.exp(-1j * (1 - a) * math.pi / 4))
            return phase * ret[..., N - 1:3 * N - 2:2]

        def _frft_last(f, a):
            if a < 0.5:
                f = _centered_ifft(f)
                a = a + 1.0
            return _frft_chirp(f, a)

        def _frft2d(x, a):
            t = _frft_last(x, a)
            return jnp.swapaxes(_frft_last(jnp.swapaxes(t, -1, -2), a), -1, -2)

        def _c1x1(x, w, b=None):
            y = jnp.einsum('nchw,oc->nohw', x, w)
            return y if b is None else y + b[None, :, None, None]

        def _c3x3(x, w, b):
            y = jax.lax.conv_general_dilated(x, w, (1, 1), 'SAME', dimension_numbers=('NCHW', 'OIHW', 'NCHW'))
            return y + b[None, :, None, None]

        def _forward(x, conv1_w, mag_s_w, mag_s_b, mag_f_w, mag_f_b, mag_w, mag_b, pha_w, pha_b, conv_0_w, conv_0_b, conv_1_w, conv_1_b, conv2_w):
            angle = 0.5
            alpha = math.cos(angle * math.pi / 2)
            N, C, H, W = x.shape
            H1, W1 = (int(H * alpha), int(W * alpha))
            x1 = _c1x1(x, conv1_w)
            C1, C0 = (C // 4, C // 4 // 3)
            x_0, x_05, x_1 = (x1[:, :C0], x1[:, C0:C1 - C0], x1[:, C1 - C0:C1])
            h0, w0 = ((H - H1) // 2, (W - W1) // 2)
            mask1 = jnp.zeros((H, W), jnp.float32).at[h0:h0 + H1, w0:w0 + W1].set(1.0)
            mask2 = 1.0 - mask1
            Fre = _frft2d(x_05.astype(C64), angle)
            mag, pha = (jnp.abs(Fre), jnp.angle(Fre))
            mag_out = _c1x1(_c3x3(mag * mask1, mag_s_w, mag_s_b) * mask1 + _c1x1(mag * mask2, mag_f_w, mag_f_b) * mask2, mag_w, mag_b)
            pha_out = _c1x1(pha, pha_w, pha_b)
            Fre_out = jax.lax.complex(mag_out * jnp.cos(pha_out), mag_out * jnp.sin(pha_out))
            ifrft = jnp.abs(_frft2d(Fre_out, -angle))
            fre = jnp.fft.rfft2(x_1)
            fm, fp = (jnp.abs(fre), jnp.angle(fre))
            mo = _c1x1(fm, conv_1_w, conv_1_b)
            po = _c1x1(fp, conv_1_w, conv_1_b)
            x_1o = jnp.fft.irfft2(jax.lax.complex(mo * jnp.cos(po), mo * jnp.sin(po)), s=(H, W))
            x_0o = _c1x1(x_0, conv_0_w, conv_0_b)
            return _c1x1(jnp.concatenate([x_0o, ifrft, x_1o], axis=1), conv2_w)
        return _forward(x, conv1_w, mag_s_w, mag_s_b, mag_f_w, mag_f_b, mag_w, mag_b, pha_w, pha_b, conv_0_w, conv_0_b, conv_1_w, conv_1_b, conv2_w)

    def _gn(v, G=32, eps=1e-5):
        B_, C_, H_, W_ = v.shape
        g = v.reshape(B_, G, C_ // G, H_, W_)
        m = jnp.mean(g, axis=(2, 3, 4), keepdims=True)
        s = jnp.var(g, axis=(2, 3, 4), keepdims=True)
        return ((g - m) / jnp.sqrt(s + eps)).reshape(v.shape)

    def _ln_c(v, eps=1e-6):
        m = jnp.mean(v, axis=1, keepdims=True)
        s = jnp.var(v, axis=1, keepdims=True)
        return (v - m) / jnp.sqrt(s + eps)

    def _ln_t(v, eps=1e-5):
        m = jnp.mean(v, axis=-1, keepdims=True)
        s = jnp.var(v, axis=-1, keepdims=True)
        return (v - m) / jnp.sqrt(s + eps)

    def _to_tokens(v):
        B_, C_, H_, W_ = v.shape
        return v.reshape(B_, C_, H_ * W_).transpose(0, 2, 1)
    def _from_tokens(t, like):
        B_, C_, H_, W_ = like.shape
        return t.transpose(0, 2, 1).reshape(B_, C_, H_, W_)

    x = x + _L0_conv_ref(_gn(x), L0_conv_w_in, L0_conv_w_dw, L0_conv_fft_w, L0_conv_w_out)
    x = x + _L1_conv_ref(_gn(x), L1_conv_conv1_w, L1_conv_mag_s_w, L1_conv_mag_s_b, L1_conv_mag_f_w, L1_conv_mag_f_b, L1_conv_mag_w, L1_conv_mag_b, L1_conv_pha_w, L1_conv_pha_b, L1_conv_conv_0_w, L1_conv_conv_0_b, L1_conv_conv_1_w, L1_conv_conv_1_b, L1_conv_conv2_w)
    return x


_drawn_inputs = setup_inputs


def setup_inputs(seed=0):
    import zlib

    import numpy as np

    out = dict(_drawn_inputs(seed))
    spreads = {}
    factors = {'L0_conv_fft_w': 8.0,
     'L1_conv_mag_s_w': 6.945,
     'L1_conv_mag_s_b': 8.0,
     'L1_conv_mag_f_w': 8.0,
     'L1_conv_mag_f_b': 24.848,
     'L1_conv_mag_w': 7.301,
     'L1_conv_mag_b': 8.0,
     'L1_conv_pha_w': 8.0,
     'L1_conv_pha_b': 64.0,
     'L1_conv_conv_0_b': 4.6,
     'L1_conv_conv_1_b': 64.0,
     'L1_conv_conv_0_w': 4.612,
     'L1_conv_conv_1_w': 5.319}
    for name, (base, spread) in spreads.items():
        noise = np.random.default_rng([zlib.crc32(name.encode()), seed]).standard_normal(out[name].shape)
        drawn = base * np.exp(spread * noise) if base else spread * noise
        out[name] = jnp.asarray(drawn.astype(out[name].dtype))
    for name, factor in factors.items():
        out[name] = (out[name] * factor).astype(out[name].dtype)
    return out
```

```python
from contextlib import ExitStack

import numpy as np

import concourse.bass as bass
from concourse import mybir

F32 = mybir.dt.float32
U32 = mybir.dt.uint32
ACT = mybir.ActivationFunctionType
ALU = mybir.AluOpType

P = 128
HALF = 96
SIDE = 128
ROWS = 8
PIX = ROWS * SIDE
PATCH = PIX // 4
STEPS = SIDE // ROWS
PADW = SIDE + 2
SLOTS = 2 * STEPS + 1
SEED = 8


def norm_stats(nc, x, agg, nb):
    rows = 16
    per = SIDE // rows
    with ExitStack() as ctx:
        xin = [ctx.enter_context(nc.sbuf_tensor(f"st_x{p}", [HALF, 2, rows * SIDE], F32)) for p in range(2)]
        stats = ctx.enter_context(nc.sbuf_tensor("st_stats", [HALF, 2, per * 4 * 6], F32))
        pair = ctx.enter_context(nc.sbuf_tensor("st_pair", [HALF, 2, 2], F32))
        loaded = [ctx.enter_context(nc.semaphore(f"st_loaded{p}")) for p in range(2)]
        read = ctx.enter_context(nc.semaphore("st_read"))
        paired = ctx.enter_context(nc.semaphore("st_paired"))
        kept = ctx.enter_context(nc.semaphore("st_kept"))
        turn = ctx.enter_context(nc.semaphore("st_turn"))
        xv = x.rearrange("b (h c) r w -> c b h (r w)", h=2)
        with nc.Block() as block:
            @block.sync
            def _(sp):
                with sp.Fori(0, nb) as b:
                    with sp.Fori(0, per // 2) as i:
                        for p in range(2):
                            sp.wait_ge(read, b * per + i * 2 + p + (SEED - 1))
                            sp.dma_start(xin[p][:], xv[:, b, :, bass.ds((i * 2 + p) * (rows * SIDE), rows * SIDE)]).then_inc(loaded[p], 16)

            @block.vector
            def _(dve):
                dve.sem_inc(read, SEED)
                with dve.Fori(0, nb) as b:
                    with dve.Fori(0, per // 2) as i:
                        for p in range(2):
                            dve.wait_ge(loaded[p], b * (per * 8) + i * 16 + 16)
                            for h in range(2):
                                for c in range(4):
                                    last = nc.vector.bn_stats(
                                        stats[:, h, bass.ds((i * 8 + p * 4 + c) * 6, 6)],
                                        xin[p][:, h, c * 512:(c + 1) * 512])
                            last.then_inc(read, 1)
                    dve.wait_ge(read, b * per + (per + SEED))
                    dve.sem_inc(turn, 1)
                    for h in range(2):
                        last = nc.vector.bn_aggr(pair[:, h], stats[:, h])
                    last.then_inc(paired, 1)
                    dve.wait_ge(paired, b + 1)
                    nc.vector.tensor_copy(agg[:, :, bass.ds(b, 1), :].rearrange("c h o t -> c h (o t)"), pair[:]).then_inc(kept, 1)
                    dve.wait_ge(kept, b + 1)


def norm_coefficients(nc, name, agg, gavg, rstd, negmr, nb, eps):
    with ExitStack() as ctx:
        dev = ctx.enter_context(nc.sbuf_tensor(name + "_dev", [HALF, 2, nb], F32))
        sq = ctx.enter_context(nc.sbuf_tensor(name + "_sq", [HALF, 2, nb], F32))
        var = ctx.enter_context(nc.sbuf_tensor(name + "_var", [HALF, 2, nb], F32))
        std = ctx.enter_context(nc.sbuf_tensor(name + "_std", [HALF, 2, nb], F32))
        gm = ctx.enter_context(nc.sbuf_tensor(name + "_gm", [HALF, 2, nb, 2], F32))
        ps1 = ctx.enter_context(nc.psum_tensor(name + "_ps1", [HALF, 4 * nb], F32))
        ps2 = ctx.enter_context(nc.psum_tensor(name + "_ps2", [HALF, 2 * nb], F32))
        v = ctx.enter_context(nc.semaphore(name + "_v"))
        mm = ctx.enter_context(nc.semaphore(name + "_mm"))
        root = ctx.enter_context(nc.semaphore(name + "_root"))
        with nc.Block() as block:
            @block.vector
            def _(dve):
                dve.wait_ge(mm, 1)
                nc.vector.tensor_copy(gm[:].rearrange("c h b t -> c (h b t)"), ps1[:]).then_inc(v, 1)
                dve.wait_ge(v, 1)
                nc.vector.tensor_tensor(dev[:], agg[:, :, :, 0], gm[:, :, :, 0], ALU.subtract).then_inc(v, 1)
                dve.wait_ge(v, 2)
                nc.vector.tensor_tensor(sq[:], dev[:], dev[:], ALU.mult).then_inc(v, 1)
                dve.wait_ge(mm, 2)
                nc.vector.tensor_tensor(var[:], gm[:, :, :, 1], ps2[:].rearrange("c (h b) -> c h b", h=2), ALU.add).then_inc(v, 1)
                dve.wait_ge(v, 4)
                nc.vector.tensor_scalar(var[:], var[:], eps, None, ALU.add).then_inc(v, 1)
                dve.wait_ge(root, 1)
                nc.vector.reciprocal(rstd[:], std[:]).then_inc(v, 1)
                dve.wait_ge(v, 6)
                nc.vector.scalar_tensor_tensor(out=negmr[:], in0=gm[:, :, :, 0], scalar=-1.0, in1=rstd[:], op0=ALU.mult, op1=ALU.mult).then_inc(v, 1)
                dve.wait_ge(v, 7)

            @block.tensor
            def _(pe):
                nc.tensor.matmul(ps1[:], gavg[:], agg[:].rearrange("c h b t -> c (h b t)"), start=True, stop=True).then_inc(mm, 1)
                pe.wait_ge(v, 3)
                nc.tensor.matmul(ps2[:], gavg[:], sq[:].rearrange("c h b -> c (h b)"), start=True, stop=True).then_inc(mm, 1)

            @block.scalar
            def _(act):
                act.wait_ge(v, 5)
                nc.scalar.activation(std[:], var[:], ACT.Sqrt).then_inc(root, 1)


def layer0(nc, x, y, w_in, w_dw, w_dwA, fft_w, w_outT, eye4, signs, agg, rstd, negmr, nb):
    npair = w_outT.shape[0] // 2
    size = [P, npair - P]
    TAPS = 9
    T = STEPS
    BLK = P // 4
    PR = ROWS // 2
    PC = SIDE // 2
    UNIT = PR * (PC + 1)
    UNITS = 16
    with ExitStack() as ctx:
        def sb(name, shape):
            return ctx.enter_context(nc.sbuf_tensor(name, shape, F32))

        def sem(name):
            return ctx.enter_context(nc.semaphore(name))

        wcur = sb("wcur", [HALF, 2, 4, P])
        dw = sb("dw", [P, 2, 2, TAPS])
        sign = sb("sign", [P, 4])
        eye = sb("eye", [P, BLK])
        mats = sb("mats", [P, 4, UNITS, P])
        fw = sb("fw", [P, 4, 4])
        fw4 = sb("fw4", [P, 4, 4])
        ball = sb("ball", [P, 4, nb])
        bcur = sb("bcur", [P, 4])
        wout = sb("wout", [P, 4, 2 * HALF])
        zero = sb("zero", [P, 1])
        xs = sb("xs", [HALF, 2, PIX])
        xr = [sb(f"xr{p}", [HALF, 2, PIX]) for p in range(2)]
        work = sb("work", [P, 4 * PATCH])
        xh = [sb(f"xh{p}", [HALF, 2, 4, PATCH]) for p in range(2)]
        hf = sb("hf", [P, 2, 4, PATCH])
        ha = sb("ha", [P, 4, 2, PATCH])
        pa = [sb(f"pa{p}", [P, 4, 2, PR + 1, PC]) for p in range(2)]
        hp = [sb(f"hp{p}", [P, 2, ROWS + 2, PADW]) for p in range(2)]
        gq = sb("gq", [P, 4, 4, UNIT])
        g = sb("g", [P, 4, 4, UNIT])
        acc = [sb(f"acc{p}", [P, 4, PIX]) for p in range(2)]
        dwA = acc[0][:, 0, 0:UNITS * TAPS].rearrange("p (u t) -> p u t", t=TAPS)
        coef = acc[1][:, 0, 0:16 * UNITS].rearrange("p (n u) -> p n u", u=UNITS)
        stats = sb("stats", [HALF, 2, SLOTS * 6])
        pair = sb("pair", [HALF, 2, 2])
        ps_in = [ctx.enter_context(nc.psum_tensor(f"ps_in{i}", [P, 512], F32)) for i in range(2)]
        ps_cv = [ctx.enter_context(nc.psum_tensor(f"ps_cv{i}", [P, UNIT], F32)) for i in range(2)]
        ps_out = [ctx.enter_context(nc.psum_tensor(f"ps_out{i}", [HALF, 512], F32)) for i in range(4)]

        const_in = sem("const_in")
        built = sem("built")
        coefs_set = sem("coefs_set")
        bias_mm = sem("bias_mm")
        w_loaded = sem("w_loaded")
        xs_in = sem("xs_in")
        xr_in = [sem(f"xr_in{p}") for p in range(2)]
        y_out = [sem(f"y_out{p}") for p in range(2)]
        pa_in = [sem(f"pa_in{p}") for p in range(2)]
        g_in = sem("g_in")
        weights_set = sem("weights_set")
        xhat_done = sem("xhat_done")
        prod_done = sem("prod_done")
        hat_done = sem("hat_done")
        hidden_done = sem("hidden_done")
        edge_done = sem("edge_done")
        conv_done = sem("conv_done")
        gelu_done = sem("gelu_done")
        first_done = sem("first_done")
        taps_done = sem("taps_done")
        gate_done = sem("gate_done")
        out_done = sem("out_done")
        y_done = sem("y_done")
        paired = sem("paired")
        kept = sem("kept")
        link = sem("link")
        turn = sem("turn")
        closed = sem("closed")

        CONV = UNITS * (T + 1)
        GATE = 4 * (T + 1)
        OUT = 4 * T + 2
        SET = 16 * UNITS
        GIN = SET * T + SET // 2

        xv = x.rearrange("b (h c) r w -> c b h (r w)", h=2)
        yv = y.rearrange("b (h c) r w -> c b h (r w)", h=2)

        def loop_steps(eng, step, tail, peeled=2):
            step(0, 0)
            step(1, 1)
            with eng.Fori(0, (T - 2 - peeled) // 2) as i:
                for q in range(2):
                    step(i * 2 + (2 + q), q)
            for t in range(T - peeled, T):
                step(t, t % 2)
            tail()

        def static(t, *values):
            return isinstance(t, int) and t in values

        with nc.Block() as block:
            @block.sync
            def _(sp):
                for q in range(2):
                    sp.sem_inc(y_out[q], 16)
                    sp.sem_inc(pa_in[q], 16)
                sp.sem_inc(g_in, 16)
                sp.wait_ge(built, 1)
                for side in range(2):
                    for c in range(2):
                        k, j0 = 2 * side + c, side * npair + c * P
                        if side == 1:
                            sp.dma_start(dw[0:size[c], c], w_dw.rearrange("(j s) t -> j s t", s=2)[j0:j0 + size[c]]).then_inc(const_in, 16)
                        sp.dma_start(fw[0:size[c], k], fft_w[j0:j0 + size[c], :]).then_inc(const_in, 16)
                for c in range(2):
                    for s in range(2):
                        sp.dma_start(wout[0:size[c], 2 * c + s], w_outT.rearrange("(j s) o -> s j o", s=2)[s, c * P:c * P + size[c], :]).then_inc(const_in, 16)
                for dst, src in ((wcur[:], w_in), (dwA, w_dwA), (sign[:], signs), (eye[:], eye4)):
                    sp.dma_start(dst, src).then_inc(const_in, 16)

                sp.wait_ge(bias_mm, 1)

                def load_x(b, t):
                    sp.wait_ge(xhat_done, b * T + t + SEED)
                    sp.dma_start(xs[:], xv[:, b, :, bass.ds(t * PIX, PIX)]).then_inc(xs_in, 16)

                def spread_patches(b, t, q):
                    sp.wait_ge(hat_done, b * (8 * T) + t * 8 + (4 + SEED))
                    sp.sem_inc(turn, 1)
                    sp.wait_ge(conv_done, b * CONV + (0 if static(t, 0) else t * UNITS - UNITS) + SEED)
                    sp.sem_inc(turn, 1)
                    sp.wait_ge(edge_done, b * (T + 1) + t + SEED)
                    for f in range(4):
                        for j in range(4):
                            sp.dma_start(pa[q][BLK * f:BLK * (f + 1), j, :, 1:PR + 1, :].rearrange("p c r w -> p c (r w)"), ha[BLK * j:BLK * (j + 1), f]).then_inc(pa_in[q], 16)

                def gather_gelu(b, t, tail=False):
                    sp.wait_ge(gate_done, b * GATE + t * 4 + SEED)
                    n = PC + 1 if tail else UNIT
                    for j in range(4):
                        sp.sem_inc(turn, 1)
                        sp.wait_ge(gelu_done, b * CONV + t * UNITS + (4 * j + 4 + SEED))
                        for px in range(2 if tail else 4):
                            sp.dma_start(g[BLK * j:BLK * (j + 1), px, :, 0:n], gq[BLK * px:BLK * (px + 1), j, :, 0:n]).then_inc(g_in, 16)

                def load_residual(b, t, q, rows=ROWS, first=False):
                    sp.wait_ge(y_out[q], b * (16 * (T // 2 + 1 - q)) + (t - q) * 8 + 16)
                    if first:
                        sp.dma_start(xr[q][:, :, SIDE:PIX], xv[:, b, :, 0:PIX - SIDE]).then_inc(xr_in[q], 16)
                    else:
                        sp.dma_start(xr[q][:, :, 0:rows * SIDE], xv[:, b, :, bass.ds(t * PIX - SIDE, rows * SIDE)]).then_inc(xr_in[q], 16)

                def store(b, t, q, rows=ROWS, first=False):
                    sp.wait_ge(y_done, b * OUT + (t * 4 + (4 if rows == ROWS else 2)) + SEED)
                    if first:
                        sp.dma_start(yv[:, b, :, 0:PIX - SIDE], xr[q][:, :, SIDE:PIX]).then_inc(y_out[q], 16)
                    else:
                        sp.dma_start(yv[:, b, :, bass.ds(t * PIX - SIDE, rows * SIDE)], xr[q][:, :, 0:rows * SIDE]).then_inc(y_out[q], 16)

                with sp.Fori(0, nb) as b:
                    sp.wait_ge(prod_done, b * (8 * T) + SEED)
                    sp.dma_start(wcur[:], w_in).then_inc(w_loaded, 16)
                    load_x(b, 0)
                    load_x(b, 1)
                    load_x(b, 2)
                    spread_patches(b, 0, 0)

                    def step(t, q):
                        if not static(t, T - 1):
                            spread_patches(b, t + 1, 1 - q)
                        load_residual(b, t, q, first=static(t, 0))
                        if not static(t, T - 3, T - 2, T - 1):
                            load_x(b, t + 3)
                        gather_gelu(b, t)
                        if not static(t, 0):
                            store(b, t - 1, 1 - q, first=static(t, 1))

                    def tail():
                        load_residual(b, T, 0, rows=1)
                        gather_gelu(b, T, tail=True)
                        store(b, T - 1, 1)
                        store(b, T, 0, rows=1)

                    loop_steps(sp, step, tail, peeled=4)
                for q in range(2):
                    sp.wait_ge(y_out[q], nb * 16 * (T // 2 + 1 - q) + 16)

            NCONST = 2 + 4 + 4 + 4

            @block.tensor
            def _(pe):
                pe.sem_inc(prod_done, SEED)
                pe.sem_inc(conv_done, SEED)
                pe.sem_inc(out_done, SEED)
                pe.wait_ge(const_in, 16 * NCONST)
                for k in range(4):
                    for h in range(2):
                        mm = nc.tensor.matmul(ps_in[0][:, k * nb:(k + 1) * nb], wcur[:, h, k, :], negmr[:, h, :], start=(h == 0), stop=(h == 1))
                mm.then_inc(bias_mm, 1)
                pe.wait_ge(built, 3)

                def product(b, t, q):
                    pe.wait_ge(xhat_done, b * T + t + (1 + SEED))
                    for k in range(4):
                        for pair in range(2):
                            pe.wait_ge(hat_done, b * (8 * T) + (t * 8 + (2 * k + pair) - 1) + SEED)
                            for h in range(2):
                                mm = nc.tensor.matmul(ps_in[pair][:], wcur[:, h, k, :], xh[q][:, h, 2 * pair:2 * pair + 2, :].rearrange("c f n -> c (f n)"), start=(h == 0), stop=(h == 1))
                            mm.then_inc(prod_done, 1)

                def conv(b, t, q, half, tail=False):
                    if not tail:
                        pe.wait_ge(pa_in[q], b * (SET * T // 2) + (t - q) * (SET // 2) + (SET + 16))
                    pe.wait_ge(edge_done, b * (T + 1) + t + (1 + SEED))
                    rows = 1 if tail else PR
                    for i in range(8 * half, 8 * half + 8):
                        pe.wait_ge(gelu_done, b * CONV + (t * UNITS + i - 1) + SEED)
                        out = ps_cv[i % 2][:, 0:rows * (PC + 1)].rearrange("p (r w) -> p r w", w=PC + 1)
                        last = 1 if tail else 3
                        for n in range(last + 1):
                            dr, dc = n // 2, n % 2
                            mm = nc.tensor.matmul(out[:, :, 1 - dc:PC + 1 - dc], mats[:, n, i, :],
                                                  pa[q][:, i // 4, (i % 4) // 2, dr:dr + rows, :],
                                                  start=(n == 0), stop=(n == last), skip_group_check=True)
                        mm.then_inc(conv_done, 1)

                def project(b, t, q, tail=False):
                    pe.wait_ge(gate_done, b * GATE + (t * 4 + 4) + SEED)
                    pe.wait_ge(y_done, b * OUT + t * 4 + SEED)
                    n = SIDE if tail else 512
                    for m in range(2):
                        for ch in range(1 if tail else 2):
                            for cs in range(4):
                                mm = nc.tensor.matmul(ps_out[2 * m + ch][:, 0:n], wout[:, cs, m * HALF:(m + 1) * HALF], acc[q][:, cs, ch * 512:ch * 512 + n], start=(cs == 0), stop=(cs == 3))
                            mm.then_inc(out_done, 1)

                with pe.Fori(0, nb) as b:
                    pe.wait_ge(weights_set, b + 1)
                    product(b, 0, 0)

                    def step(t, q):
                        if not static(t, T - 1):
                            product(b, t + 1, 1 - q)
                        conv(b, t, q, 0)
                        if not static(t, 0):
                            project(b, t - 1, 1 - q)
                        conv(b, t, q, 1)

                    def tail():
                        conv(b, T, 0, 0, tail=True)
                        conv(b, T, 0, 1, tail=True)
                        project(b, T - 1, 1)
                        project(b, T, 0, tail=True)

                    loop_steps(pe, step, tail)

            @block.scalar
            def _(act):
                act.sem_inc(hat_done, SEED)
                act.sem_inc(edge_done, SEED)
                act.sem_inc(gelu_done, SEED)
                act.sem_inc(first_done, SEED)
                act.wait_ge(built, 3)

                def evacuate(b, t, q):
                    act.wait_ge(pa_in[1 - q], b * (SET * T // 2) + (t + q) * (SET // 2) + 16)
                    for k in range(4):
                        if k >= 2:
                            act.wait_ge(hidden_done, b * (2 * T) + (t * 2 - 2 + (k - 2) + 1) + SEED)
                        for pair in range(2):
                            act.wait_ge(prod_done, b * (8 * T) + (t * 8 + 2 * k + pair + 1) + SEED)
                            for e in range(2):
                                f = 2 * pair + e
                                dst = ha[:, f, k, :] if k < 2 else hf[:, k - 2, f, :]
                                if f == 0:
                                    last = nc.scalar.activation(dst, ps_in[pair][:, e * PATCH:(e + 1) * PATCH], ACT.Identity, bias=bcur[:, k:k + 1], scale=fw4[:, k, f:f + 1])
                                else:
                                    last = nc.scalar.activation(dst, ps_in[pair][:, e * PATCH:(e + 1) * PATCH], ACT.Copy, scale=fw4[:, k, f:f + 1])
                            last.then_inc(hat_done, 1)

                def edge(b, t, q, first=False, tail=False):
                    if first:
                        act.wait_ge(conv_done, b * CONV + SEED)
                        act.wait_ge(taps_done, b * GATE + SEED)
                        nc.scalar.copy(hp[q][:, :, 0:2, :], zero[:].unsqueeze(2).unsqueeze(3).broadcast_to([P, 2, 2, PADW]))
                        nc.scalar.copy(pa[q][:, :, :, 0, :].rearrange("p j c w -> p (j c) w"), zero[:].unsqueeze(2).broadcast_to([P, 8, PC])).then_inc(edge_done, 1)
                        return
                    act.wait_ge(hidden_done, b * (2 * T) + t * 2 + SEED)
                    act.wait_ge(taps_done, b * GATE + (t * 4 - 4) + SEED)
                    act.wait_ge(pa_in[1 - q], b * (SET * T // 2) + (t + q) * (SET // 2) + 16)
                    act.wait_ge(conv_done, b * CONV + (t * UNITS - UNITS) + SEED)
                    nc.scalar.copy(hp[q][:, :, 0:2, :], hp[1 - q][:, :, ROWS:ROWS + 2, :])
                    if tail:
                        nc.scalar.copy(hp[q][:, :, 2, :], zero[:].unsqueeze(2).broadcast_to([P, 2, PADW]))
                    nc.scalar.copy(pa[q][:, :, :, 0, :].rearrange("p j c w -> p (j c) w"), pa[1 - q][:, :, :, PR, :].rearrange("p j c w -> p (j c) w")).then_inc(edge_done, 1)

                def first_taps(b, t, q, some, rows=ROWS):
                    act.wait_ge(edge_done, b * (T + 1) + t + (1 + SEED))
                    if rows == ROWS:
                        act.wait_ge(hidden_done, b * (2 * T) + t * 2 + (2 + SEED))
                    act.wait_ge(out_done, b * OUT + (0 if static(t, 0, 1) else t * 4 - 4) + SEED)
                    for cs in some:
                        nc.scalar.activation(acc[q][:, cs, 0:rows * SIDE].rearrange("p (r w) -> p r w", w=SIDE), hp[q][:, cs // 2, 0:rows, 0:SIDE],
                                             ACT.Copy, scale=dw[:, cs // 2, cs % 2, 0:1]).then_inc(first_done, 1)

                def gelu(b, t, units, tail=False):
                    act.wait_ge(g_in, b * GIN + t * SET + 16)
                    n = PC + 1 if tail else UNIT
                    for i in units:
                        act.wait_ge(conv_done, b * CONV + (t * UNITS + i + 1) + SEED)
                        nc.scalar.activation(gq[:, i // 4, i % 4, 0:n], ps_cv[i % 2][:, 0:n], ACT.Gelu).then_inc(gelu_done, 1)

                with act.Fori(0, nb) as b:
                    act.wait_ge(weights_set, b + 1)
                    evacuate(b, 0, 0)
                    edge(b, 0, 0, first=True)
                    first_taps(b, 0, 0, range(4))

                    def step(t, q):
                        last = static(t, T - 1)
                        if not last:
                            evacuate(b, t + 1, 1 - q)
                        gelu(b, t, range(8))
                        edge(b, t + 1, 1 - q, tail=last)
                        for cs in range(4):
                            gelu(b, t, range(8 + 2 * cs, 10 + 2 * cs))
                            first_taps(b, t + 1, 1 - q, [cs], rows=1 if last else ROWS)

                    def tail():
                        gelu(b, T, range(UNITS), tail=True)

                    loop_steps(act, step, tail)

            @block.vector
            def _(dve):
                for s in (xhat_done, hidden_done, taps_done, gate_done, y_done):
                    dve.sem_inc(s, SEED)
                dve.memset(dw[:], 0.0)
                dve.memset(fw[:], 0.0)
                dve.memset(zero[:], 0.0)
                dve.memset(xr[0][:], 0.0)
                for p in range(2):
                    dve.memset(hp[p][:], 0.0)
                dve.memset(wout[:], 0.0).then_inc(built, 1)
                dve.wait_ge(const_in, 16 * NCONST)
                dve.wait_ge(bias_mm, 1)
                for k in range(4):
                    nc.vector.tensor_scalar(ball[:, k, :], ps_in[0][:, k * nb:(k + 1) * nb], fw[:, k, 0:1], None, ALU.mult)
                nc.vector.tensor_scalar(fw4[:], fw[:], 0.25, None, ALU.mult).then_inc(built, 1)
                added = 0
                for n in range(16):
                    dr, dc, qy, qx = n >> 3, n >> 2 & 1, n >> 1 & 1, n & 1
                    begun = False
                    for r in range(4):
                        ky, kx = 2 * dr + r // 2 - qy, 2 * dc + r % 2 - qx
                        if not (0 <= ky < 3 and 0 <= kx < 3):
                            continue
                        w = dwA[:, :, 3 * ky + kx]
                        if not begun:
                            nc.vector.tensor_scalar(coef[:, n, :], w, sign[:, r:r + 1], None, ALU.mult).then_inc(coefs_set, 1)
                        else:
                            dve.wait_ge(coefs_set, added)
                            nc.vector.scalar_tensor_tensor(out=coef[:, n, :], in0=w, scalar=sign[:, r:r + 1], in1=coef[:, n, :], op0=ALU.mult, op1=ALU.add).then_inc(coefs_set, 1)
                        begun = True
                        added += 1
                dve.wait_ge(coefs_set, added)
                for n in range(16):
                    last = nc.vector.tensor_tensor(mats[:, n // 4, :, (n % 4) * BLK:(n % 4 + 1) * BLK], coef[:, n, :].unsqueeze(2).broadcast_to([P, UNITS, BLK]),
                                                   eye[:].unsqueeze(1).broadcast_to([P, UNITS, BLK]), ALU.mult)
                last.then_inc(built, 1)
                dve.wait_ge(built, 3)

                n_link = [0]

                def mark(ins):
                    n_link[0] += 1
                    return ins.then_inc(link, 1)

                def linked():
                    dve.wait_ge(link, n_link[0])

                def close():
                    dve.sem_inc(closed, 1)
                    linked()
                    dve.sem_clear(link)
                    n_link[0] = 0

                def frequencies(b, t, q):
                    dve.wait_ge(xs_in, b * (16 * T) + t * 16 + 16)
                    v = xs[:].rearrange("c h (r two w) -> c h r two w", two=2, w=SIDE)
                    o = xh[q][:].rearrange("c h (fy fx) n -> c fy fx h n", fx=2)
                    sums = work[0:HALF, :].rearrange("c (h n) -> c h n", h=2)
                    u = sums.rearrange("c h (n two) -> c h n two", two=2)
                    if not static(t, 0, 1):
                        dve.wait_ge(prod_done, b * (8 * T) + (t * 8 - 8) + SEED)
                    for fy, op in ((0, ALU.add), (1, ALU.subtract)):
                        mark(nc.vector.tensor_tensor(sums.rearrange("c h (r w) -> c h r w", w=SIDE), v[:, :, :, 0, :], v[:, :, :, 1, :], op))
                        linked()
                        nc.vector.tensor_tensor(o[:, fy, 0], u[:, :, :, 0], u[:, :, :, 1], ALU.add)
                        last = nc.vector.tensor_tensor(o[:, fy, 1], u[:, :, :, 0], u[:, :, :, 1], ALU.subtract)
                        if fy == 0:
                            mark(last)
                            linked()
                    last.then_inc(xhat_done, 1)
                    dve.wait_ge(xhat_done, b * T + t + (1 + SEED))

                def hidden(b, t, q, c):
                    dve.wait_ge(hat_done, b * (8 * T) + (t * 8 + 2 * (c + 2) + 2) + SEED)
                    ht = work[:].rearrange("p (f n) -> p f n", f=4)
                    lo, hi = hf[:, c, 0:2, :], hf[:, c, 2:4, :]
                    nc.vector.tensor_tensor(ht[:, 0:2, :], lo, hi, ALU.add)
                    mark(nc.vector.tensor_tensor(ht[:, 2:4, :], lo, hi, ALU.subtract))
                    linked()
                    if c == 0:
                        dve.wait_ge(edge_done, b * (T + 1) + t + SEED)
                    u = ht.rearrange("p (py fx) (r n) -> p py fx r n", fx=2, n=PC)
                    o = hp[q][:, c, 2:ROWS + 2, 1:SIDE + 1].rearrange("p (r py) (n px) -> p py px r n", py=2, px=2)
                    nc.vector.tensor_tensor(o[:, :, 0], u[:, :, 0], u[:, :, 1], ALU.add)
                    nc.vector.tensor_tensor(o[:, :, 1], u[:, :, 0], u[:, :, 1], ALU.subtract).then_inc(hidden_done, 1)
                    dve.wait_ge(hidden_done, b * (2 * T) + (t * 2 + c + 1) + SEED)

                def taps(b, t, q, c, rows=ROWS):
                    made = [0, 0]
                    for tap in range(1, TAPS):
                        h = hp[q][:, c, tap // 3:tap // 3 + rows, tap % 3:tap % 3 + SIDE]
                        for s in range(2):
                            cs = 2 * c + s
                            if tap == 1:
                                dve.wait_ge(first_done, b * GATE + (t * 4 + cs + 1) + SEED)
                            else:
                                dve.wait_ge(link, made[s])
                            out = acc[q][:, cs, 0:rows * SIDE].rearrange("p (r w) -> p r w", w=SIDE)
                            ins = nc.vector.scalar_tensor_tensor(out=out, in0=h, scalar=dw[:, c, s, tap:tap + 1], in1=out, op0=ALU.mult, op1=ALU.add)
                            if tap < TAPS - 1:
                                mark(ins)
                                made[s] = n_link[0]
                            else:
                                ins.then_inc(taps_done, 1)

                def gates(b, t, q, tail=False):
                    dve.wait_ge(taps_done, b * GATE + t * 4 + (4 + SEED))
                    dve.wait_ge(g_in, b * GIN + t * SET + ((SET // 2 if tail else SET) + 16))
                    for cs in range(4):
                        for qx in range(2):
                            lo = 1 - qx
                            if tail:
                                d = acc[q][:, cs, 0:SIDE].rearrange("p (w two) -> p w two", two=2)[:, :, lo]
                                s = g[:, qx, cs, lo:lo + PC]
                            else:
                                d = acc[q][:, cs, :].rearrange("p (r qy w two) -> p qy r w two", qy=2, w=PC, two=2)[:, :, :, :, lo]
                                s = g[:, qx:4:2, cs, :].rearrange("p qy (r w) -> p qy r w", w=PC + 1)[:, :, :, lo:lo + PC]
                            last = nc.vector.tensor_tensor(d, s, d, ALU.mult)
                        last.then_inc(gate_done, 1)

                def residual(b, t, q, tail=False, first=False):
                    n = SIDE if tail else 512
                    dve.wait_ge(xr_in[q], b * (16 * (T // 2 + 1 - q)) + (t - q) * 8 + 16)
                    parts = [(m, ch) for m in range(2) for ch in range(1 if tail else 2)]
                    summed = []

                    def records(i):
                        m, ch = parts[i]
                        lo = SIDE if (first and ch == 0) else 0
                        dve.wait_ge(link, summed[i])
                        nc.vector.bn_stats(stats[:, m, bass.ds((t * 2 + ch) * 6, 6)],
                                           xr[q][:, m, ch * 512 + lo:ch * 512 + n]).then_inc(y_done, 1)

                    for i, (m, ch) in enumerate(parts):
                        dve.wait_ge(out_done, b * OUT + (t * 4 + i + 1) + SEED)
                        s = slice(ch * 512, ch * 512 + n)
                        mark(nc.vector.tensor_tensor(xr[q][:, m, s], ps_out[2 * m + ch][:, 0:n], xr[q][:, m, s], ALU.add))
                        summed.append(n_link[0])
                        if i:
                            records(i - 1)
                    records(len(parts) - 1)

                with dve.Fori(0, nb) as b:
                    dve.wait_ge(w_loaded, b * 16 + 16)
                    dve.wait_ge(hat_done, b * (8 * T) + SEED)
                    for h in range(2):
                        nc.vector.tensor_scalar(wcur[:, h], wcur[:, h], rstd[:, h, bass.ds(b, 1)], None, ALU.mult)
                    nc.vector.tensor_copy(bcur[:], ball[:, :, bass.ds(b, 1)].rearrange("p k o -> p (k o)")).then_inc(weights_set, 1)
                    frequencies(b, 0, 0)
                    frequencies(b, 1, 1)
                    for c in range(2):
                        hidden(b, 0, 0, c)
                    close()

                    def step(t, q):
                        last = static(t, T - 1)
                        if not static(t, 0):
                            gates(b, t - 1, 1 - q)
                        if not static(t, T - 2, T - 1):
                            frequencies(b, t + 2, q)
                        if not last:
                            for c in range(2):
                                hidden(b, t + 1, 1 - q, c)
                        for c in range(2):
                            taps(b, t, q, c)
                        if not static(t, 0):
                            residual(b, t - 1, 1 - q, first=static(t, 1))
                        close()

                    def tail():
                        gates(b, T - 1, 1)
                        for c in range(2):
                            taps(b, T, 0, c, rows=1)
                        residual(b, T - 1, 1)
                        gates(b, T, 0, tail=True)
                        residual(b, T, 0, tail=True)
                        dve.wait_ge(y_done, b * OUT + (OUT + SEED))
                        dve.sem_inc(closed, 1)
                        for h in range(2):
                            last = nc.vector.bn_aggr(pair[:, h], stats[:, h])
                        last.then_inc(paired, 1)
                        dve.wait_ge(paired, b + 1)
                        nc.vector.tensor_copy(agg[:, :, bass.ds(b, 1), :].rearrange("c h o t -> c h (o t)"), pair[:]).then_inc(kept, 1)
                        dve.wait_ge(kept, b + 1)
                        close()

                    loop_steps(dve, step, tail)


def layer1_in(nc, y, w1T, w0T, b0, rstd, negmr, x1, cat, nb):
    rows = 16
    px = rows * SIDE
    per = SIDE // rows
    C1 = w1T.shape[1]
    C0 = C1 // 3
    with ExitStack() as ctx:
        def sb(name, shape):
            return ctx.enter_context(nc.sbuf_tensor(name, shape, F32))

        def sem(name):
            return ctx.enter_context(nc.semaphore(name))

        w1 = sb("w1", [HALF, 2, C1])
        w1cur = sb("w1cur", [HALF, 2, C1])
        w0 = sb("w0", [C0, C0])
        b0s = sb("b0s", [C0, 1])
        ball = sb("b1all", [C1, nb])
        bcur = sb("b1cur", [C1, 1])
        yin = [sb(f"yin{p}", [HALF, 2, px]) for p in range(2)]
        z = [sb(f"z{p}", [C1, px]) for p in range(2)]
        z0 = [sb(f"z0{p}", [C0, px]) for p in range(2)]
        ps = [ctx.enter_context(nc.psum_tensor(f"ps_1{i}", [C1, 512], F32)) for i in range(4)]
        ps0 = [ctx.enter_context(nc.psum_tensor(f"ps_0{i}", [C0, 512], F32)) for i in range(4)]
        const_in = sem("in_const")
        bias_mm = sem("in_bias_mm")
        weights_set = sem("in_weights")
        pe_turn = sem("in_pe_turn")
        loaded = [sem(f"in_loaded{p}") for p in range(2)]
        stored = [sem(f"in_stored{p}") for p in range(2)]
        stored0 = [sem(f"in_stored0{p}") for p in range(2)]
        mm1 = sem("in_mm1")
        z_done = sem("in_z")
        mm0 = sem("in_mm0")
        z0_done = sem("in_z0")
        yv = y.rearrange("b (h c) r w -> c b h (r w)", h=2)
        x1v = x1.rearrange("b c r w -> c b (r w)")
        catv = cat.rearrange("b c r w -> c b (r w)")

        with nc.Block() as block:
            @block.sync
            def _(sp):
                for q in range(2):
                    sp.sem_inc(stored[q], 16)
                    sp.sem_inc(stored0[q], 16)
                sp.dma_start(w1[:], w1T.rearrange("(h c) o -> c h o", h=2)).then_inc(const_in, 16)
                sp.dma_start(w0[:], w0T).then_inc(const_in, 16)
                sp.dma_start(b0s[:], b0).then_inc(const_in, 16)
                with sp.Fori(0, nb) as b:
                    with sp.Fori(0, per // 2) as i:
                        for q in range(2):
                            sp.wait_ge(mm1, b * (4 * per) + (i * 8 + 4 * q - 4) + SEED)
                            sp.dma_start(yin[q][:], yv[:, b, :, bass.ds((i * 2 + q) * px, px)]).then_inc(loaded[q], 16)

            @block.tensor
            def _(pe):
                pe.sem_inc(mm1, SEED)
                pe.sem_inc(mm0, SEED)
                pe.wait_ge(const_in, 48)
                for h in range(2):
                    mm = nc.tensor.matmul(ps[0][:, 0:nb], w1[:, h, :], negmr[:, h, :], start=(h == 0), stop=(h == 1))
                mm.then_inc(bias_mm, 1)
                with pe.Fori(0, nb) as b:
                    pe.wait_ge(weights_set, b + 2)
                    pe.sem_inc(pe_turn, 1)
                    with pe.Fori(0, per // 2) as i:
                        for q in range(2):
                            pe.wait_ge(loaded[q], b * (8 * per) + i * 16 + 16)
                            for c in range(4):
                                pe.wait_ge(z_done, b * (4 * per) + (i * 8 + 4 * q + c - 3) + SEED)
                                for h in range(2):
                                    mm = nc.tensor.matmul(ps[c][:], w1cur[:, h, :], yin[q][:, h, c * 512:(c + 1) * 512], start=(h == 0), stop=(h == 1))
                                mm.then_inc(mm1, 1)
                            for c in range(4):
                                pe.wait_ge(z_done, b * (4 * per) + (i * 8 + 4 * q + c + 1) + SEED)
                                pe.wait_ge(z0_done, b * (4 * per) + (i * 8 + 4 * q + c - 3) + SEED)
                                pe.sem_inc(pe_turn, 1)
                                nc.tensor.matmul(ps0[c][:], w0[:], z[q][0:C0, c * 512:(c + 1) * 512], start=True, stop=True).then_inc(mm0, 1)

            @block.scalar
            def _(act):
                act.sem_inc(z_done, SEED)
                with act.Fori(0, nb) as b:
                    act.wait_ge(weights_set, b + 2)
                    with act.Fori(0, per // 2) as i:
                        for q in range(2):
                            act.wait_ge(stored[q], b * (8 * per) + i * 16 + 16)
                            act.wait_ge(mm0, b * (4 * per) + (i * 8 + 4 * q - 4) + SEED)
                            for c in range(4):
                                act.wait_ge(mm1, b * (4 * per) + (i * 8 + 4 * q + c + 1) + SEED)
                                nc.scalar.activation(z[q][:, c * 512:(c + 1) * 512], ps[c][:], ACT.Identity, bias=bcur[:, 0:1]).then_inc(z_done, 1)
                            act.wait_ge(z_done, b * (4 * per) + (i * 8 + 4 * q + 4) + SEED)
                            act.dma_start(x1v[C0:C1, b, bass.ds((i * 2 + q) * px, px)], z[q][C0:C1, :]).then_inc(stored[q], 16)
                            act.wait_ge(z0_done, b * (4 * per) + (i * 8 + 4 * q + 4) + SEED)
                            act.dma_start(catv[0:C0, b, bass.ds((i * 2 + q) * px, px)], z0[q][:]).then_inc(stored0[q], 16)
                for q in range(2):
                    act.wait_ge(stored[q], nb * 8 * per + 16)
                    act.wait_ge(stored0[q], nb * 8 * per + 16)

            @block.vector
            def _(dve):
                dve.sem_inc(z0_done, SEED)
                dve.wait_ge(bias_mm, 1)
                dve.wait_ge(const_in, 48)
                nc.vector.tensor_copy(ball[:], ps[0][:, 0:nb]).then_inc(weights_set, 1)
                dve.wait_ge(weights_set, 1)
                with dve.Fori(0, nb) as b:
                    dve.wait_ge(mm1, b * (4 * per) + SEED)
                    dve.wait_ge(z_done, b * (4 * per) + SEED)
                    for h in range(2):
                        nc.vector.tensor_scalar(w1cur[:, h], w1[:, h], rstd[:, h, bass.ds(b, 1)], None, ALU.mult)
                    nc.vector.tensor_copy(bcur[:], ball[:, bass.ds(b, 1)]).then_inc(weights_set, 1)
                    with dve.Fori(0, per // 2) as i:
                        for q in range(2):
                            dve.wait_ge(stored0[q], b * (8 * per) + i * 16 + 16)
                            for c in range(4):
                                dve.wait_ge(mm0, b * (4 * per) + (i * 8 + 4 * q + c + 1) + SEED)
                                nc.vector.tensor_scalar(z0[q][:, c * 512:(c + 1) * 512], ps0[c][:], b0s[:, 0:1], None, ALU.add).then_inc(z0_done, 1)


def layer1_out(nc, y, cat, w2T, out, nb):
    rows = 16
    px = rows * SIDE
    per = SIDE // rows
    C1 = w2T.shape[0]
    with ExitStack() as ctx:
        def sb(name, shape):
            return ctx.enter_context(nc.sbuf_tensor(name, shape, F32))

        def sem(name):
            return ctx.enter_context(nc.semaphore(name))

        w2 = sb("w2", [C1, 2 * HALF])
        yin = [sb(f"oy{p}", [HALF, 2, px]) for p in range(2)]
        cin = [sb(f"oc{p}", [C1, px]) for p in range(2)]
        oo = [sb(f"oo{p}", [HALF, 2, px]) for p in range(2)]
        ps = [ctx.enter_context(nc.psum_tensor(f"ps_o{i}", [HALF, 512], F32)) for i in range(8)]
        const_in = sem("out_const")
        y_in = [sem(f"out_y{p}") for p in range(2)]
        c_in = [sem(f"out_c{p}") for p in range(2)]
        stored = [sem(f"out_stored{p}") for p in range(2)]
        mm = sem("out_mm")
        summed = sem("out_sum")
        yv = y.rearrange("b (h c) r w -> c b h (r w)", h=2)
        ov = out.rearrange("b (h c) r w -> c b h (r w)", h=2)
        catv = cat.rearrange("b c r w -> c b (r w)")

        with nc.Block() as block:
            @block.sync
            def _(sp):
                sp.dma_start(w2[:], w2T).then_inc(const_in, 16)
                with sp.Fori(0, nb) as b:
                    with sp.Fori(0, per // 2) as i:
                        for q in range(2):
                            sp.wait_ge(summed, b * (8 * per) + (i * 16 + 8 * q - 8) + SEED)
                            sp.dma_start(cin[q][:], catv[:, b, bass.ds((i * 2 + q) * px, px)]).then_inc(c_in[q], 16)
                            sp.dma_start(yin[q][:], yv[:, b, :, bass.ds((i * 2 + q) * px, px)]).then_inc(y_in[q], 16)

            @block.tensor
            def _(pe):
                pe.wait_ge(const_in, 16)
                with pe.Fori(0, nb) as b:
                    with pe.Fori(0, per // 2) as i:
                        for q in range(2):
                            pe.wait_ge(c_in[q], b * (8 * per) + i * 16 + 16)
                            for m in range(2):
                                for c in range(4):
                                    pe.wait_ge(summed, b * (8 * per) + (i * 16 + 8 * q + 4 * m + c - 7) + SEED)
                                    nc.tensor.matmul(ps[4 * m + c][:], w2[:, m * HALF:(m + 1) * HALF], cin[q][:, c * 512:(c + 1) * 512], start=True, stop=True).then_inc(mm, 1)

            @block.vector
            def _(dve):
                dve.sem_inc(summed, SEED)
                with dve.Fori(0, nb) as b:
                    with dve.Fori(0, per // 2) as i:
                        for q in range(2):
                            dve.wait_ge(y_in[q], b * (8 * per) + i * 16 + 16)
                            dve.wait_ge(stored[q], b * (8 * per) + i * 16 + 16)
                            for m in range(2):
                                for c in range(4):
                                    dve.wait_ge(mm, b * (8 * per) + (i * 16 + 8 * q + 4 * m + c + 1))
                                    s = slice(c * 512, (c + 1) * 512)
                                    nc.vector.tensor_tensor(oo[q][:, m, s], ps[4 * m + c][:], yin[q][:, m, s], ALU.add).then_inc(summed, 1)

            @block.scalar
            def _(act):
                for q in range(2):
                    act.sem_inc(stored[q], 16)
                with act.Fori(0, nb) as b:
                    with act.Fori(0, per // 2) as i:
                        for q in range(2):
                            act.wait_ge(summed, b * (8 * per) + (i * 16 + 8 * q + 8) + SEED)
                            act.dma_start(ov[:, b, :, bass.ds((i * 2 + q) * px, px)], oo[q][:]).then_inc(stored[q], 16)
                for q in range(2):
                    act.wait_ge(stored[q], nb * 8 * per + 16)


FRAC = 16 * SIDE
HALFW = SIDE // 2 + 1
FOUR = 16 * HALFW
ALL = FRAC + FOUR
PI = float(np.pi)
TWO_PI = 2 * PI
PI_A = 6.28125
PI_B = float(np.float32(np.round((TWO_PI - PI_A) * 2**22) / 2**22))
PI_C = TWO_PI - PI_A - PI_B
ROUND = 1.5 * 2.0**23
PI_MAX = 3.1415925
TINY = 1e-30


def layer1_planes(nc, x1, cat, consts, mixes, biases, mask, scratch, nb):
    polar1, polar2, back1, back2 = scratch
    GROUPS = 24
    with ExitStack() as ctx:
        def sb(name, shape):
            return ctx.enter_context(nc.sbuf_tensor(name, shape, F32))

        def sem(name):
            return ctx.enter_context(nc.semaphore(name))

        c_frac, c_ifrac, c_f1, c_f2, c_i1, c_i2 = consts
        frac = sb("frac", [P, 2, 2 * SIDE])
        ifrac = sb("ifrac", [P, 2, 2 * SIDE])
        four1 = sb("four1", [P, 2 * SIDE])
        four2 = sb("four2", [P, 2, 2 * HALFW])
        inv1 = sb("inv1", [P, 2, 2 * SIDE])
        inv2 = sb("inv2", [HALFW, 2, SIDE])
        mix = sb("mix", [P, 13, P])
        bias = sb("bias", [P, 5])
        msk = sb("msk", [P, 18, SIDE])
        xp = sb("xp", [P, 32, SIDE])
        tb = [sb(f"tb{q}", [P, 2 * SIDE]) for q in range(2)]
        sq = [sb(f"sq{q}", [P, 2 * SIDE]) for q in range(2)]
        ri = sb("ri", [P, 2, ALL])
        t = sb("t", [P, 4, ALL])
        gm = sb("gm", [P, 2, ALL])
        mp = sb("mp", [P, 18, PADW])
        mo = sb("mo", [P, 2, ALL])
        z = sb("z", [P, 2, ALL])
        ps_a = [ctx.enter_context(nc.psum_tensor(f"ps_a{q}", [P, 512], F32)) for q in range(2)]
        ps_b = [ctx.enter_context(nc.psum_tensor(f"ps_b{q}", [P, 512], F32)) for q in range(2)]
        ps_c = [ctx.enter_context(nc.psum_tensor(f"ps_c{q}", [P, 512], F32)) for q in range(4)]

        const_in = sem("pl_const")
        zeroed = sem("pl_zeroed")
        xp_in = sem("xp_in")
        polar_out = sem("polar_out")
        gm_in = sem("gm_in")
        back_out = sem("back_out")
        z_in = sem("z_in")
        cat_out = sem("cat_out")
        pass1 = sem("pass1")
        between = sem("between")
        pass2 = sem("pass2")
        taken = sem("taken")
        squared = sem("squared")
        pol_a = sem("pol_a")
        pol_v = sem("pol_v")
        inv_v = sem("inv_v")
        inv_a = sem("inv_a")
        mix_mm = sem("mix_mm")
        mix_ev = sem("mix_ev")
        mix_v = sem("mix_v")
        mix_a = sem("mix_a")
        link = sem("pl_link")
        closed = sem("pl_closed")

        def turns(eng, forward, inverse, mixes_):
            forward(0, 0)
            forward(1, 32)
            mixes_(0)
            with eng.Fori(1, nb - 1) as i:
                forward(i + 1, i * 64)
                inverse(i - 1, i * 64 + 32)
                mixes_(i)
            inverse(nb - 2, (nb - 1) * 64)
            mixes_(nb - 1)
            inverse(nb - 1, (nb - 1) * 64 + 32)

        by_row = "c h w -> h c w"
        by_block = "c (k r) w -> k c (r w)"

        with nc.Block() as block:
            @block.sync
            def _(sp):
                for s in (polar_out, back_out, cat_out, gm_in, z_in):
                    sp.sem_inc(s, 16)
                for dst, src in ((frac, c_frac), (ifrac, c_ifrac), (four1, c_f1), (four2, c_f2), (inv1, c_i1), (inv2, c_i2), (mix, mixes), (bias, biases), (msk, mask)):
                    sp.dma_start(dst[:], src).then_inc(const_in, 16)
                sp.wait_ge(zeroed, 1)

                def load_planes(i):
                    for c in range(0, 32, 8):
                        sp.dma_start(xp[:, c:c + 8, :], x1[i].rearrange(by_row)[:, 16 + c:24 + c]).then_inc(xp_in, 16)

                def store_polar(i):
                    sp.wait_ge(pol_a, i * 4 + (4 + SEED))
                    sp.wait_ge(gm_in, i * 96 + 16)
                    for k in range(2):
                        sp.dma_start(polar1[k].rearrange(by_row), t[:, k, 0:FRAC].rearrange("h (c w) -> h c w", w=SIDE)).then_inc(polar_out, 16)
                        sp.dma_start(polar2[k].rearrange(by_row), t[:, k, FRAC:ALL].rearrange("h (c w) -> h c w", w=HALFW)).then_inc(polar_out, 16)

                def load_mix(i):
                    sp.wait_ge(polar_out, i * 64 + (64 + 16))
                    for k in range(2):
                        sp.dma_start(gm[:, k, 0:FRAC], polar1[k].rearrange(by_block, k=8)).then_inc(gm_in, 16)
                        sp.dma_start(gm[:, k, FRAC:ALL], polar2[k].rearrange(by_block, k=8)).then_inc(gm_in, 16)
                    rows = polar1[0].rearrange("c (k r) w -> k c r w", k=8)
                    sp.dma_start(mp[16:P, 0, 1:SIDE + 1], rows[0:7, :, 15, :]).then_inc(gm_in, 16)
                    sp.dma_start(mp[0:P - 16, 17, 1:SIDE + 1], rows[1:8, :, 0, :]).then_inc(gm_in, 16)

                def forward(i, base):
                    store_polar(i)
                    if isinstance(i, int) and i == 0:
                        sp.wait_ge(pass1, 32 + SEED)
                        load_planes(1)
                        load_mix(0)

                def inverse(i, base):
                    sp.wait_ge(inv_a, i + (1 + SEED))
                    sp.dma_start(cat[i].rearrange(by_row)[:, 16:48], xp[:]).then_inc(cat_out, 16)

                def mixes_(i):
                    if not (isinstance(i, int) and i >= nb - 1):
                        sp.wait_ge(mix_mm, i * GROUPS + (GROUPS + SEED))
                        load_mix(i + 1)
                    sp.wait_ge(mix_v, i * 7 + (7 + SEED))
                    sp.wait_ge(z_in, i * 96 + 16)
                    for src, k in ((t[:, 2], 0), (mo[:, 1], 1)):
                        sp.dma_start(back1[k].rearrange(by_block, k=8), src[:, 0:FRAC]).then_inc(back_out, 16)
                        sp.dma_start(back2[k].rearrange(by_block, k=8), src[:, FRAC:ALL]).then_inc(back_out, 16)
                    sp.wait_ge(back_out, i * 64 + (64 + 16))
                    for k in range(2):
                        for c in (0, 8):
                            sp.dma_start(z[:, k, c * SIDE:(c + 8) * SIDE].rearrange("h (c w) -> h c w", w=SIDE), back1[k].rearrange(by_row)[:, c:c + 8]).then_inc(z_in, 16)
                        sp.dma_start(z[:, k, FRAC:ALL].rearrange("h (c w) -> h c w", w=HALFW), back2[k].rearrange(by_row)).then_inc(z_in, 16)

                load_planes(0)
                forward(0, 0)
                forward(1, 32)
                sp.wait_ge(pass1, 64 + SEED)
                load_planes(2)
                mixes_(0)
                with sp.Fori(1, nb - 2) as i:
                    forward(i + 1, 0)
                    inverse(i - 1, 0)
                    sp.wait_ge(cat_out, i * 16 + 16)
                    load_planes(i + 2)
                    mixes_(i)
                forward(nb - 1, 0)
                inverse(nb - 3, 0)
                mixes_(nb - 2)
                inverse(nb - 2, 0)
                mixes_(nb - 1)
                inverse(nb - 1, 0)
                sp.wait_ge(cat_out, nb * 16 + 16)

            @block.tensor
            def _(pe):
                for s in (pass1, pass2, mix_mm):
                    pe.sem_inc(s, SEED)
                pe.wait_ge(const_in, 16 * 9)

                def transform(base, first, second):
                    for n in range(33):
                        if n < 32:
                            pe.wait_ge(between, base + (n - 1 + SEED))
                            first(n, ps_a[n % 2]).then_inc(pass1, 1)
                        if n > 0:
                            c = n - 1
                            pe.wait_ge(between, base + (c + 1 + SEED))
                            pe.wait_ge(taken, base + (c - 1 + SEED))
                            second(c, ps_b[c % 2]).then_inc(pass2, 1)

                def forward(i, base):
                    pe.wait_ge(xp_in, i * 64 + 64)

                    def first(c, out):
                        return nc.tensor.matmul(out[:, 0:256], xp[:, c, :], frac[:, 0, :] if c < 16 else four1[:], start=True, stop=True)

                    def second(c, out):
                        w = frac if c < 16 else four2
                        n = w.shape[2]
                        for k in range(2):
                            mm = nc.tensor.matmul(out[:, 0:n], tb[c % 2][:, k * SIDE:(k + 1) * SIDE], w[:, k, :], start=(k == 0), stop=(k == 1))
                        return mm

                    transform(base, first, second)

                def inverse(i, base):
                    pe.wait_ge(z_in, i * 96 + (96 + 16))

                    def first(c, out):
                        n, at, w = (SIDE, c * SIDE, ifrac) if c < 16 else (HALFW, FRAC + (c - 16) * HALFW, inv1)
                        for k in range(2):
                            mm = nc.tensor.matmul(out[0:n, 0:256], z[:, k, at:at + n], w[:, k, :], start=(k == 0), stop=(k == 1))
                        return mm

                    def second(c, out):
                        n, w, m = (P, ifrac, 256) if c < 16 else (HALFW, inv2, SIDE)
                        for k in range(2):
                            mm = nc.tensor.matmul(out[:, 0:m], tb[c % 2][0:n, k * SIDE:(k + 1) * SIDE], w[:, k, :], start=(k == 0), stop=(k == 1))
                        return mm

                    transform(base, first, second)

                def mixes_(i):
                    pe.wait_ge(gm_in, i * 96 + (96 + 16))
                    q4 = FOUR // 4

                    def group(n, products):
                        pe.wait_ge(mix_ev, i * GROUPS + (n - 3 + SEED))
                        for k, (w, src) in enumerate(products):
                            shape = src.shape
                            cols = int(np.prod(shape[1:]))
                            mm = nc.tensor.matmul(ps_c[n % 4][:, 0:cols], mix[:, w, :], src, start=(k == 0), stop=(k == len(products) - 1))
                        mm.then_inc(mix_mm, 1)

                    for j in range(4):
                        group(j, [(9, gm[:, 0, j * 512:(j + 1) * 512])])
                    pe.wait_ge(mix_v, i * 7 + (1 + SEED))
                    for j in range(4):
                        group(4 + j, [(tap, mp[:, 4 * j + tap // 3:4 * j + tap // 3 + 4, tap % 3:tap % 3 + SIDE]) for tap in range(9)])
                    for j in range(4):
                        group(8 + j, [(11, gm[:, 1, j * 512:(j + 1) * 512])])
                    for j in range(4):
                        group(12 + j, [(12, gm[:, 1, FRAC + j * q4:FRAC + (j + 1) * q4])])
                    for j in range(4):
                        group(16 + j, [(12, gm[:, 0, FRAC + j * q4:FRAC + (j + 1) * q4])])
                    for j in range(4):
                        pe.wait_ge(mix_v, i * 7 + (2 + j + SEED))
                        group(20 + j, [(10, t[:, 2, j * 512:(j + 1) * 512])])

                turns(pe, forward, inverse, mixes_)

            @block.scalar
            def _(act):
                for s in (between, squared, pol_a, inv_a, mix_ev, mix_a):
                    act.sem_inc(s, SEED)
                act.wait_ge(const_in, 16 * 9)

                def copy_between(base, rows, extra=None):
                    for n in range(32):
                        act.wait_ge(pass1, base + (n + 1 + SEED))
                        act.wait_ge(pass2, base + (n - 1 + SEED))
                        m = rows(n)
                        nc.scalar.copy(tb[n % 2][0:m], ps_a[n % 2][0:m, 0:256]).then_inc(between, 1)
                        if extra and n > 0:
                            extra(n - 1)
                    if extra:
                        extra(31)

                def forward(i, base):
                    copy_between(base, lambda n: P)
                    act.wait_ge(taken, base + (32 + SEED))
                    act.wait_ge(polar_out, i * 64 + 16)
                    nc.scalar.activation(t[:, 0, :], ri[:, 0, :], ACT.Abs)
                    nc.scalar.activation(t[:, 1, :], ri[:, 1, :], ACT.Abs).then_inc(pol_a, 1)
                    act.wait_ge(pol_v, i * 3 + (1 + SEED))
                    nc.scalar.activation(t[:, 1, :], t[:, 3, :], ACT.Arctan).then_inc(pol_a, 1)
                    act.wait_ge(pol_v, i * 3 + (2 + SEED))
                    nc.scalar.activation(ri[:, 0, :], ri[:, 0, :], ACT.Square)
                    nc.scalar.activation(ri[:, 1, :], ri[:, 1, :], ACT.Square).then_inc(pol_a, 1)
                    act.wait_ge(pol_v, i * 3 + (3 + SEED))
                    nc.scalar.activation(t[:, 0, :], t[:, 0, :], ACT.Sqrt).then_inc(pol_a, 1)

                def inverse(i, base):
                    def square(c):
                        if c < 16:
                            act.wait_ge(pass2, base + (c + 1 + SEED))
                            act.wait_ge(taken, base + (c - 1 + SEED))
                            nc.scalar.activation(sq[c % 2][:], ps_b[c % 2][:, 0:256], ACT.Square).then_inc(squared, 1)

                    copy_between(base, lambda n: P if n < 16 else HALFW, square)
                    act.wait_ge(inv_v, i + (1 + SEED))
                    nc.scalar.activation(xp[:, 0:16, :], xp[:, 0:16, :], ACT.Sqrt).then_inc(inv_a, 1)

                def mixes_(i):
                    act.wait_ge(back_out, i * 64 + 16)
                    q4 = FOUR // 4

                    def take(n, dst, k):
                        act.wait_ge(mix_mm, i * GROUPS + (n + 1 + SEED))
                        m = dst.shape[1]
                        nc.scalar.activation(dst, ps_c[n % 4][:, 0:m], ACT.Identity, bias=bias[:, k:k + 1]).then_inc(mix_ev, 1)

                    for j in range(4):
                        take(j, t[:, 2, j * 512:(j + 1) * 512], 1)
                    for j in range(4):
                        take(4 + j, t[:, 3, j * 512:(j + 1) * 512], 0)
                    for j in range(4):
                        take(8 + j, mo[:, 1, j * 512:(j + 1) * 512], 3)
                    for k in range(2):
                        for j in range(4):
                            take(12 + 4 * k + j, mo[:, 1 - k, FRAC + j * q4:FRAC + (j + 1) * q4], 4)
                    for j in range(4):
                        take(20 + j, mo[:, 0, j * 512:(j + 1) * 512], 2)
                    act.wait_ge(mix_v, i * 7 + (6 + SEED))
                    nc.scalar.activation(mo[:, 1, :], mo[:, 1, :], ACT.Sin)
                    nc.scalar.activation(t[:, 2, :], t[:, 2, :], ACT.Sin).then_inc(mix_a, 1)

                turns(act, forward, inverse, mixes_)

            @block.vector
            def _(dve):
                for s in (taken, pol_v, inv_v, mix_v):
                    dve.sem_inc(s, SEED)
                dve.memset(mp[:], 0.0).then_inc(zeroed, 1)
                dve.wait_ge(zeroed, 1)
                n_link = [0]

                def op(ins):
                    n_link[0] += 1
                    ins.then_inc(link, 1)
                    dve.wait_ge(link, n_link[0])

                def close():
                    dve.sem_inc(closed, 1)
                    dve.wait_ge(link, n_link[0])
                    dve.sem_clear(link)
                    n_link[0] = 0

                def forward(i, base):
                    for c in range(32):
                        dve.wait_ge(pass2, base + (c + 1 + SEED))
                        n, at = (SIDE, c * SIDE) if c < 16 else (HALFW, FRAC + (c - 16) * HALFW)
                        nc.vector.tensor_copy(ri[:, :, at:at + n], ps_b[c % 2][:, 0:2 * n].rearrange("p (k n) -> p k n", k=2)).then_inc(taken, 1)
                    re, im = ri[:, 0, :], ri[:, 1, :]
                    t0, t1, t2, t3 = (t[:, k, :] for k in range(4))
                    v = nc.vector
                    dve.wait_ge(pol_a, i * 4 + (1 + SEED))
                    dve.wait_ge(back_out, (i - 1) * 64 + 16 if not isinstance(i, int) else max(i - 1, 0) * 64 + 16)
                    op(v.tensor_tensor(t2, t0, t1, ALU.max))
                    op(v.tensor_tensor(t3, t0, t1, ALU.min))
                    op(v.tensor_tensor(t0, t1, t0, ALU.is_gt))
                    op(v.tensor_scalar(t2, t2, TINY, None, ALU.max))
                    op(v.reciprocal(t2, t2))
                    v.tensor_tensor(t3, t3, t2, ALU.mult).then_inc(pol_v, 1)
                    dve.wait_ge(pol_a, i * 4 + (2 + SEED))
                    dve.wait_ge(pol_v, i * 3 + (1 + SEED))
                    op(v.tensor_scalar(t2, t1, -2.0, PI / 2, ALU.mult, ALU.add))
                    op(v.tensor_tensor(t2, t2, t0, ALU.mult))
                    op(v.tensor_tensor(t1, t1, t2, ALU.add))
                    op(v.tensor_scalar(t2, t1, -2.0, PI, ALU.mult, ALU.add))
                    op(v.scalar_tensor_tensor(out=t2, in0=re, scalar=0.0, in1=t2, op0=ALU.is_lt, op1=ALU.mult))
                    op(v.tensor_tensor(t1, t1, t2, ALU.add))
                    op(v.tensor_scalar(t2, im, 0.0, -2.0, ALU.is_lt, ALU.mult))
                    v.scalar_tensor_tensor(out=t1, in0=t2, scalar=1.0, in1=t1, op0=ALU.add, op1=ALU.mult).then_inc(pol_v, 1)
                    dve.wait_ge(pol_a, i * 4 + (3 + SEED))
                    v.tensor_tensor(t0, re, im, ALU.add).then_inc(pol_v, 1)
                    dve.wait_ge(pol_v, i * 3 + (3 + SEED))
                    close()

                def inverse(i, base):
                    dve.wait_ge(cat_out, i * 16 + 16)
                    for c in range(32):
                        if c < 16:
                            dve.wait_ge(squared, i * 16 + (c + 1 + SEED))
                            ins = nc.vector.tensor_tensor(xp[:, c, :], sq[c % 2][:, 0:SIDE], sq[c % 2][:, SIDE:256], ALU.add)
                        else:
                            dve.wait_ge(pass2, base + (c + 1 + SEED))
                            ins = nc.vector.tensor_copy(xp[:, c, :], ps_b[c % 2][:, 0:SIDE])
                        ins.then_inc(taken, 1)
                    dve.wait_ge(taken, base + (32 + SEED))
                    dve.sem_inc(inv_v, 1)

                def mixes_(i):
                    v = nc.vector
                    dve.wait_ge(gm_in, i * 96 + (96 + 16))
                    op(v.tensor_tensor(mp[:, 1:17, 1:SIDE + 1], gm[:, 0, 0:FRAC].rearrange("p (r w) -> p r w", w=SIDE), msk[:, 1:17, :], ALU.mult))
                    v.tensor_tensor(mp[:, 0:18:17, 1:SIDE + 1], mp[:, 0:18:17, 1:SIDE + 1], msk[:, 0:18:17, :], ALU.mult).then_inc(mix_v, 1)
                    for j in range(4):
                        dve.wait_ge(mix_ev, i * GROUPS + (5 + j + SEED))
                        dve.sem_inc(closed, 1)
                        s = slice(j * 512, (j + 1) * 512)
                        v.copy_predicated(t[:, 2, s], msk[:, 1 + 4 * j:5 + 4 * j, :].bitcast(U32).rearrange("p r w -> p (r w)"), t[:, 3, s]).then_inc(mix_v, 1)
                    dve.wait_ge(mix_ev, i * GROUPS + (24 + SEED))
                    a, u, w = mo[:, 1, :], t[:, 2, :], t[:, 3, :]
                    op(v.tensor_scalar(u, a, 1 / TWO_PI, ROUND, ALU.mult, ALU.add))
                    op(v.tensor_scalar(u, u, ROUND, None, ALU.subtract))
                    for part in (PI_A, PI_B, PI_C):
                        op(v.scalar_tensor_tensor(out=a, in0=u, scalar=-part, in1=a, op0=ALU.mult, op1=ALU.add))
                    op(v.tensor_scalar(a, a, PI_MAX, -PI_MAX, ALU.min, ALU.max))
                    op(v.tensor_scalar(u, a, PI / 2, None, ALU.add))
                    op(v.tensor_scalar(w, u, PI, -TWO_PI, ALU.is_gt, ALU.mult))
                    op(v.tensor_tensor(u, u, w, ALU.add))
                    v.tensor_scalar(u, u, PI_MAX, -PI_MAX, ALU.min, ALU.max).then_inc(mix_v, 1)
                    dve.wait_ge(mix_a, i + (1 + SEED))
                    op(v.tensor_tensor(u, u, mo[:, 0, :], ALU.mult))
                    v.tensor_tensor(a, a, mo[:, 0, :], ALU.mult).then_inc(mix_v, 1)
                    dve.wait_ge(mix_v, i * 7 + (7 + SEED))
                    close()

                turns(dve, forward, inverse, mixes_)


N = SIDE


def fractional_matrix(a):
    alpha = a * np.pi / 2
    tana2, sina = np.tan(alpha / 2), np.sin(alpha)
    up = np.zeros((N, 2 * N - 1))
    up[:, ::2] = np.eye(N)
    sinc = np.sinc(np.arange(-(2 * N - 3), 2 * N - 2) / 2.0)
    fi = np.stack([np.convolve(r, sinc)[2 * N - 3:4 * N - 4] for r in up])
    n = np.arange(-2 * N + 2, 2 * N - 1).astype(np.float64)
    chirp = np.exp(-1j * np.pi / N * tana2 / 4 * n**2)
    pad = np.zeros((N, N - 1))
    fp = np.concatenate([pad, fi, pad], axis=1) * chirp
    c = np.pi / N / sina / 4
    m = np.arange(-(4 * N - 4), 4 * N - 3).astype(np.float64)
    kern = np.exp(1j * c * m**2)
    ret = np.stack([np.convolve(r, kern)[4 * N - 4:8 * N - 7] for r in fp]) * np.sqrt(c / np.pi)
    return (np.exp(-1j * (1 - a) * np.pi / 4) * chirp * ret)[:, N - 1:3 * N - 2:2]


def centered_inverse_matrix():
    shft = (np.arange(N) + N // 2) % N
    return (np.fft.ifft(np.eye(N)[:, shft], axis=-1) * np.sqrt(N))[:, np.argsort(shft)]


def real_pair(m):
    return np.stack([np.concatenate([m.real, m.imag], 1), np.concatenate([-m.imag, m.real], 1)], 1).astype(np.float32)


def shape_constants():
    frac = fractional_matrix(0.5)
    ifrac = centered_inverse_matrix() @ fractional_matrix(0.5)
    k = np.arange(N)
    turn = np.outer(k, k) % N
    cos, sin = np.cos(2 * np.pi * turn / N), np.sin(2 * np.pi * turn / N)
    cos[turn % (N // 2) == N // 4] = 0
    sin[turn % (N // 2) == 0] = 0
    four = cos - 1j * sin
    twice = np.full((HALFW, 1), 2.0)
    twice[0] = twice[-1] = 1
    inv2 = np.stack([twice * cos[:HALFW], -twice * sin[:HALFW]], 1) / N**2
    mask = np.zeros((N + 2, N), np.float32)
    inner = int(N * np.cos(0.5 * np.pi / 2))
    lo = (N - inner) // 2
    mask[lo + 1:lo + 1 + inner, lo:lo + inner] = 1
    mask = np.stack([mask[16 * b:16 * b + 18] for b in range(8) for _ in range(16)])
    return {
        "c_frac": real_pair(frac),
        "c_ifrac": real_pair(ifrac),
        "c_four1": real_pair(four)[:, 0],
        "c_four2": real_pair(four[:, :HALFW]),
        "c_inv1": real_pair(four.conj()),
        "c_inv2": inv2.astype(np.float32),
        "c_mask": mask,
        "c_eye4": np.tile(np.eye(P // 4, dtype=np.float32), (4, 1)),
        "c_sign": np.repeat(np.array([[(-1.0) ** (fy * ry + fx * rx) for ry in range(2) for rx in range(2)] for fy in range(2) for fx in range(2)], np.float32), P // 4, 0),
        "c_gavg": np.kron(np.eye(16), np.full((6, 6), 1 / 6)).astype(np.float32),
    }


def laid_out(w):
    def blocks(m):
        out = np.zeros((P, P), np.float32)
        for b in range(8):
            out[16 * b:16 * b + 16, 16 * b:16 * b + 16] = m.T
        return out

    s = w["L1_conv_mag_s_w"]
    mats = [s[:, :, t // 3, t % 3] for t in range(9)] + [w["L1_conv_mag_f_w"], w["L1_conv_mag_w"], w["L1_conv_pha_w"], w["L1_conv_conv_1_w"]]
    rows = [w["L1_conv_mag_s_b"], w["L1_conv_mag_f_b"], w["L1_conv_mag_b"], w["L1_conv_pha_b"], w["L1_conv_conv_1_b"]]
    dw = w["L0_conv_w_dw"].reshape(-1, 2, 9)
    half = np.zeros((2 * P, 2, 9), np.float32)
    half[:dw.shape[0] // 2] = dw[:dw.shape[0] // 2]
    half = half.reshape(2, 4, P // 4, 2, 9).transpose(2, 1, 0, 3, 4)
    hid = w["L0_conv_w_in"].shape[0]
    w_in = np.zeros((2 * HALF, 2, 2 * P), np.float32)
    for side in range(2):
        w_in[:, side, :hid // 2] = w["L0_conv_w_in"][side * (hid // 2):(side + 1) * (hid // 2), :, 0, 0].T
    return {
        "w_dwA": np.tile(half.reshape(P // 4, 16, 9), (4, 1, 1)),
        "w_in": w_in.reshape(2, HALF, 4, P).transpose(1, 0, 2, 3),
        "w_dw": w["L0_conv_w_dw"].reshape(-1, 9),
        "fft_w": w["L0_conv_fft_w"].reshape(-1, 4),
        "w_outT": w["L0_conv_w_out"][:, :, 0, 0].T,
        "w1T": w["L1_conv_conv1_w"].T,
        "w0T": w["L1_conv_conv_0_w"].T,
        "b0": w["L1_conv_conv_0_b"].reshape(-1, 1),
        "w2T": w["L1_conv_conv2_w"].T,
        "mixes": np.stack([blocks(m) for m in mats], 1),
        "biases": np.stack([np.tile(r, 8) for r in rows], 1),
    }


def program(nc, d, out, nb):
    y = nc.dram_tensor("y_scratch", [nb, 192, SIDE, SIDE], F32).ap()
    x1 = nc.dram_tensor("x1_scratch", [nb, 48, SIDE, SIDE], F32).ap()
    cat = nc.dram_tensor("cat_scratch", [nb, 48, SIDE, SIDE], F32).ap()
    scratch = [nc.dram_tensor(f"{n}_scratch", [2, 16, SIDE, w], F32).ap() for n, w in (("polar1", SIDE), ("polar2", HALFW), ("back1", SIDE), ("back2", HALFW))]
    with ExitStack() as ctx:
        gavg = ctx.enter_context(nc.sbuf_tensor("gavg", [HALF, HALF], F32))
        agg = ctx.enter_context(nc.sbuf_tensor("agg", [HALF, 2, nb, 2], F32))
        rstd = ctx.enter_context(nc.sbuf_tensor("rstd", [HALF, 2, nb], F32))
        negmr = ctx.enter_context(nc.sbuf_tensor("negmr", [HALF, 2, nb], F32))
        loaded = ctx.enter_context(nc.semaphore("first_loaded"))
        with nc.Block() as block:
            @block.sync
            def _(sp):
                sp.dma_start(gavg[:], d["c_gavg"]).then_inc(loaded, 16)
                sp.wait_ge(loaded, 16)
        norm_stats(nc, d["x"], agg, nb)
        norm_coefficients(nc, "norm0", agg, gavg, rstd, negmr, nb, 1e-5)
        layer0(nc, d["x"], y, d["w_in"], d["w_dw"], d["w_dwA"], d["fft_w"], d["w_outT"], d["c_eye4"], d["c_sign"], agg, rstd, negmr, nb)
        norm_coefficients(nc, "norm1", agg, gavg, rstd, negmr, nb, 1e-5)
        layer1_in(nc, y, d["w1T"], d["w0T"], d["b0"], rstd, negmr, x1, cat, nb)
    consts = [d[n] for n in ("c_frac", "c_ifrac", "c_four1", "c_four2", "c_inv1", "c_inv2")]
    layer1_planes(nc, x1, cat, consts, d["mixes"], d["biases"], d["c_mask"], scratch, nb)
    layer1_out(nc, y, cat, d["w2T"], out, nb)


def kernel(**inputs):
    import concourse.bacc as _bacc
    from concourse.bass_utils import run_bass_kernel_spmd as _run

    w = {name: np.asarray(a) for name, a in inputs.items()}
    arrays = {"x": w["x"], **laid_out(w), **shape_constants()}
    arrays = {name: np.ascontiguousarray(a) for name, a in arrays.items()}
    nc = _bacc.Bacc("TRN2", target_bir_lowering=False, num_devices=1)
    d = {name: nc.dram_tensor(name, list(a.shape), F32, kind="ExternalInput").ap() for name, a in arrays.items()}
    out = nc.dram_tensor("out", list(w["x"].shape), F32, kind="ExternalOutput").ap()
    program(nc, d, out, w["x"].shape[0])
    r = _run(nc, [arrays], core_ids=[0])
    return r.results[0]["out"]
```

```python
from contextlib import ExitStack

import numpy as np

import concourse.bass as bass
from concourse import mybir

F32 = mybir.dt.float32
U32 = mybir.dt.uint32
ACT = mybir.ActivationFunctionType
ALU = mybir.AluOpType

P = 128
HALF = 96
SIDE = 128
ROWS = 8
PIX = ROWS * SIDE
PATCH = PIX // 4
STEPS = SIDE // ROWS
PADW = SIDE + 2
SLOTS = 2 * STEPS + 1
SEED = 8


def norm_stats(nc, x, agg, nb):
    rows = 16
    per = SIDE // rows
    with ExitStack() as ctx:
        xin = [ctx.enter_context(nc.sbuf_tensor(f"st_x{p}", [HALF, 2, rows * SIDE], F32)) for p in range(2)]
        stats = ctx.enter_context(nc.sbuf_tensor("st_stats", [HALF, 2, per * 4 * 6], F32))
        pair = ctx.enter_context(nc.sbuf_tensor("st_pair", [HALF, 2, 2], F32))
        loaded = [ctx.enter_context(nc.semaphore(f"st_loaded{p}")) for p in range(2)]
        read = ctx.enter_context(nc.semaphore("st_read"))
        paired = ctx.enter_context(nc.semaphore("st_paired"))
        kept = ctx.enter_context(nc.semaphore("st_kept"))
        turn = ctx.enter_context(nc.semaphore("st_turn"))
        xv = x.rearrange("b (h c) r w -> c b h (r w)", h=2)
        with nc.Block() as block:
            @block.sync
            def _(sp):
                with sp.Fori(0, nb) as b:
                    with sp.Fori(0, per // 2) as i:
                        for p in range(2):
                            sp.wait_ge(read, b * per + i * 2 + p + (SEED - 1))
                            sp.dma_start(xin[p][:], xv[:, b, :, bass.ds((i * 2 + p) * (rows * SIDE), rows * SIDE)]).then_inc(loaded[p], 16)

            @block.vector
            def _(dve):
                dve.sem_inc(read, SEED)
                with dve.Fori(0, nb) as b:
                    with dve.Fori(0, per // 2) as i:
                        for p in range(2):
                            dve.wait_ge(loaded[p], b * (per * 8) + i * 16 + 16)
                            for h in range(2):
                                for c in range(4):
                                    last = nc.vector.bn_stats(
                                        stats[:, h, bass.ds((i * 8 + p * 4 + c) * 6, 6)],
                                        xin[p][:, h, c * 512:(c + 1) * 512])
                            last.then_inc(read, 1)
                    dve.wait_ge(read, b * per + (per + SEED))
                    dve.sem_inc(turn, 1)
                    for h in range(2):
                        last = nc.vector.bn_aggr(pair[:, h], stats[:, h])
                    last.then_inc(paired, 1)
                    dve.wait_ge(paired, b + 1)
                    nc.vector.tensor_copy(agg[:, :, bass.ds(b, 1), :].rearrange("c h o t -> c h (o t)"), pair[:]).then_inc(kept, 1)
                    dve.wait_ge(kept, b + 1)


def norm_coefficients(nc, name, agg, gavg, rstd, negmr, nb, eps):
    with ExitStack() as ctx:
        dev = ctx.enter_context(nc.sbuf_tensor(name + "_dev", [HALF, 2, nb], F32))
        sq = ctx.enter_context(nc.sbuf_tensor(name + "_sq", [HALF, 2, nb], F32))
        var = ctx.enter_context(nc.sbuf_tensor(name + "_var", [HALF, 2, nb], F32))
        std = ctx.enter_context(nc.sbuf_tensor(name + "_std", [HALF, 2, nb], F32))
        gm = ctx.enter_context(nc.sbuf_tensor(name + "_gm", [HALF, 2, nb, 2], F32))
        ps1 = ctx.enter_context(nc.psum_tensor(name + "_ps1", [HALF, 4 * nb], F32))
        ps2 = ctx.enter_context(nc.psum_tensor(name + "_ps2", [HALF, 2 * nb], F32))
        v = ctx.enter_context(nc.semaphore(name + "_v"))
        mm = ctx.enter_context(nc.semaphore(name + "_mm"))
        root = ctx.enter_context(nc.semaphore(name + "_root"))
        with nc.Block() as block:
            @block.vector
            def _(dve):
                dve.wait_ge(mm, 1)
                nc.vector.tensor_copy(gm[:].rearrange("c h b t -> c (h b t)"), ps1[:]).then_inc(v, 1)
                dve.wait_ge(v, 1)
                nc.vector.tensor_tensor(dev[:], agg[:, :, :, 0], gm[:, :, :, 0], ALU.subtract).then_inc(v, 1)
                dve.wait_ge(v, 2)
                nc.vector.tensor_tensor(sq[:], dev[:], dev[:], ALU.mult).then_inc(v, 1)
                dve.wait_ge(mm, 2)
                nc.vector.tensor_tensor(var[:], gm[:, :, :, 1], ps2[:].rearrange("c (h b) -> c h b", h=2), ALU.add).then_inc(v, 1)
                dve.wait_ge(v, 4)
                nc.vector.tensor_scalar(var[:], var[:], eps, None, ALU.add).then_inc(v, 1)
                dve.wait_ge(root, 1)
                nc.vector.reciprocal(rstd[:], std[:]).then_inc(v, 1)
                dve.wait_ge(v, 6)
                nc.vector.scalar_tensor_tensor(out=negmr[:], in0=gm[:, :, :, 0], scalar=-1.0, in1=rstd[:], op0=ALU.mult, op1=ALU.mult).then_inc(v, 1)
                dve.wait_ge(v, 7)

            @block.tensor
            def _(pe):
                nc.tensor.matmul(ps1[:], gavg[:], agg[:].rearrange("c h b t -> c (h b t)"), start=True, stop=True).then_inc(mm, 1)
                pe.wait_ge(v, 3)
                nc.tensor.matmul(ps2[:], gavg[:], sq[:].rearrange("c h b -> c (h b)"), start=True, stop=True).then_inc(mm, 1)

            @block.scalar
            def _(act):
                act.wait_ge(v, 5)
                nc.scalar.activation(std[:], var[:], ACT.Sqrt).then_inc(root, 1)


def layer0(nc, x, y, w_in, w_dw, w_dwA, fft_w, w_outT, eye4, signs, agg, rstd, negmr, nb):
    npair = w_outT.shape[0] // 2
    size = [P, npair - P]
    TAPS = 9
    T = STEPS
    BLK = P // 4
    PR = ROWS // 2
    PC = SIDE // 2
    UNIT = PR * (PC + 1)
    UNITS = 16
    with ExitStack() as ctx:
        def sb(name, shape):
            return ctx.enter_context(nc.sbuf_tensor(name, shape, F32))

        def sem(name):
            return ctx.enter_context(nc.semaphore(name))

        wcur = sb("wcur", [HALF, 2, 4, P])
        dw = sb("dw", [P, 2, 2, TAPS])
        sign = sb("sign", [P, 4])
        eye = sb("eye", [P, BLK])
        mats = sb("mats", [P, 4, UNITS, P])
        fw = sb("fw", [P, 4, 4])
        fw4 = sb("fw4", [P, 4, 4])
        ball = sb("ball", [P, 4, nb])
        bcur = sb("bcur", [P, 4])
        wout = sb("wout", [P, 4, 2 * HALF])
        zero = sb("zero", [P, 1])
        xs = sb("xs", [HALF, 2, PIX])
        xr = [sb(f"xr{p}", [HALF, 2, PIX]) for p in range(2)]
        work = sb("work", [P, 4 * PATCH])
        xh = [sb(f"xh{p}", [HALF, 2, 4, PATCH]) for p in range(2)]
        hf = sb("hf", [P, 2, 4, PATCH])
        ha = sb("ha", [P, 4, 2, PATCH])
        pa = [sb(f"pa{p}", [P, 4, 2, PR + 1, PC]) for p in range(2)]
        hp = [sb(f"hp{p}", [P, 2, ROWS + 2, PADW]) for p in range(2)]
        gq = sb("gq", [P, 4, 4, UNIT])
        g = sb("g", [P, 4, 4, UNIT])
        acc = [sb(f"acc{p}", [P, 4, PIX]) for p in range(2)]
        dwA = acc[0][:, 0, 0:UNITS * TAPS].rearrange("p (u t) -> p u t", t=TAPS)
        coef = acc[1][:, 0, 0:16 * UNITS].rearrange("p (n u) -> p n u", u=UNITS)
        stats = sb("stats", [HALF, 2, SLOTS * 6])
        pair = sb("pair", [HALF, 2, 2])
        ps_in = [ctx.enter_context(nc.psum_tensor(f"ps_in{i}", [P, 512], F32)) for i in range(2)]
        ps_cv = [ctx.enter_context(nc.psum_tensor(f"ps_cv{i}", [P, UNIT], F32)) for i in range(2)]
        ps_out = [ctx.enter_context(nc.psum_tensor(f"ps_out{i}", [HALF, 512], F32)) for i in range(4)]

        const_in = sem("const_in")
        built = sem("built")
        coefs_set = sem("coefs_set")
        bias_mm = sem("bias_mm")
        w_loaded = sem("w_loaded")
        xs_in = sem("xs_in")
        xr_in = [sem(f"xr_in{p}") for p in range(2)]
        y_out = [sem(f"y_out{p}") for p in range(2)]
        pa_in = [sem(f"pa_in{p}") for p in range(2)]
        g_in = sem("g_in")
        weights_set = sem("weights_set")
        xhat_done = sem("xhat_done")
        prod_done = sem("prod_done")
        hat_done = sem("hat_done")
        hidden_done = sem("hidden_done")
        edge_done = sem("edge_done")
        conv_done = sem("conv_done")
        gelu_done = sem("gelu_done")
        first_done = sem("first_done")
        taps_done = sem("taps_done")
        gate_done = sem("gate_done")
        out_done = sem("out_done")
        y_done = sem("y_done")
        paired = sem("paired")
        kept = sem("kept")
        link = sem("link")
        turn = sem("turn")
        closed = sem("closed")

        CONV = UNITS * (T + 1)
        GATE = 4 * (T + 1)
        OUT = 4 * T + 2
        SET = 16 * UNITS
        GIN = SET * T + SET // 2

        xv = x.rearrange("b (h c) r w -> c b h (r w)", h=2)
        yv = y.rearrange("b (h c) r w -> c b h (r w)", h=2)

        def loop_steps(eng, step, tail, peeled=2):
            step(0, 0)
            step(1, 1)
            with eng.Fori(0, (T - 2 - peeled) // 2) as i:
                for q in range(2):
                    step(i * 2 + (2 + q), q)
            for t in range(T - peeled, T):
                step(t, t % 2)
            tail()

        def images(eng, image):
            with eng.Fori(0, nb - 1) as b:
                image(b, False)
            image(nb - 1, True)

        def static(t, *values):
            return isinstance(t, int) and t in values

        with nc.Block() as block:
            @block.sync
            def _(sp):
                for q in range(2):
                    sp.sem_inc(y_out[q], 16)
                    sp.sem_inc(pa_in[q], 16)
                sp.sem_inc(g_in, 16)
                sp.wait_ge(built, 1)
                for side in range(2):
                    for c in range(2):
                        k, j0 = 2 * side + c, side * npair + c * P
                        if side == 1:
                            sp.dma_start(dw[0:size[c], c], w_dw.rearrange("(j s) t -> j s t", s=2)[j0:j0 + size[c]]).then_inc(const_in, 16)
                        sp.dma_start(fw[0:size[c], k], fft_w[j0:j0 + size[c], :]).then_inc(const_in, 16)
                for c in range(2):
                    for s in range(2):
                        sp.dma_start(wout[0:size[c], 2 * c + s], w_outT.rearrange("(j s) o -> s j o", s=2)[s, c * P:c * P + size[c], :]).then_inc(const_in, 16)
                for dst, src in ((wcur[:], w_in), (dwA, w_dwA), (sign[:], signs), (eye[:], eye4)):
                    sp.dma_start(dst, src).then_inc(const_in, 16)

                sp.wait_ge(bias_mm, 1)

                def load_x(b, t):
                    sp.wait_ge(xhat_done, b * T + t + SEED)
                    image, t = (b + 1, t - T) if isinstance(t, int) and t >= T else (b, t)
                    sp.dma_start(xs[:], xv[:, image, :, bass.ds(t * PIX, PIX)]).then_inc(xs_in, 16)

                def load_weights(b):
                    sp.wait_ge(prod_done, b * (8 * T) + SEED)
                    sp.dma_start(wcur[:], w_in).then_inc(w_loaded, 16)

                def spread_patches(b, t, q):
                    sp.wait_ge(hat_done, b * (8 * T) + t * 8 + (4 + SEED))
                    sp.sem_inc(turn, 1)
                    sp.wait_ge(conv_done, b * CONV + (0 if static(t, 0) else t * UNITS - UNITS) + SEED)
                    sp.sem_inc(turn, 1)
                    sp.wait_ge(edge_done, b * (T + 1) + t + SEED)
                    for f in range(4):
                        for j in range(4):
                            sp.dma_start(pa[q][BLK * f:BLK * (f + 1), j, :, 1:PR + 1, :].rearrange("p c r w -> p c (r w)"), ha[BLK * j:BLK * (j + 1), f]).then_inc(pa_in[q], 16)

                def gather_gelu(b, t, tail=False):
                    sp.wait_ge(gate_done, b * GATE + t * 4 + SEED)
                    n = PC + 1 if tail else UNIT
                    for j in range(4):
                        sp.sem_inc(turn, 1)
                        sp.wait_ge(gelu_done, b * CONV + t * UNITS + (4 * j + 4 + SEED))
                        for px in range(2 if tail else 4):
                            sp.dma_start(g[BLK * j:BLK * (j + 1), px, :, 0:n], gq[BLK * px:BLK * (px + 1), j, :, 0:n]).then_inc(g_in, 16)

                def load_residual(b, t, q, rows=ROWS, first=False):
                    sp.wait_ge(y_out[q], b * (16 * (T // 2 + 1 - q)) + (t - q) * 8 + 16)
                    if first:
                        sp.dma_start(xr[q][:, :, SIDE:PIX], xv[:, b, :, 0:PIX - SIDE]).then_inc(xr_in[q], 16)
                    else:
                        sp.dma_start(xr[q][:, :, 0:rows * SIDE], xv[:, b, :, bass.ds(t * PIX - SIDE, rows * SIDE)]).then_inc(xr_in[q], 16)

                def store(b, t, q, rows=ROWS, first=False):
                    sp.wait_ge(y_done, b * OUT + (t * 4 + (4 if rows == ROWS else 2)) + SEED)
                    if first:
                        sp.dma_start(yv[:, b, :, 0:PIX - SIDE], xr[q][:, :, SIDE:PIX]).then_inc(y_out[q], 16)
                    else:
                        sp.dma_start(yv[:, b, :, bass.ds(t * PIX - SIDE, rows * SIDE)], xr[q][:, :, 0:rows * SIDE]).then_inc(y_out[q], 16)

                def image(b, last):
                    def step(t, q):
                        if not (last and static(t, T - 1)):
                            spread_patches(b, t + 1, 1 - q)
                        load_residual(b, t, q, first=static(t, 0))
                        if not (last and static(t, T - 3, T - 2, T - 1)):
                            load_x(b, t + 3)
                        if static(t, T - 2) and not last:
                            load_weights(b + 1)
                        gather_gelu(b, t)
                        if not static(t, 0):
                            store(b, t - 1, 1 - q, first=static(t, 1))

                    def tail():
                        load_residual(b, T, 0, rows=1)
                        gather_gelu(b, T, tail=True)
                        store(b, T - 1, 1)
                        store(b, T, 0, rows=1)

                    loop_steps(sp, step, tail, peeled=4)

                load_weights(0)
                for t in range(3):
                    load_x(0, t)
                spread_patches(0, 0, 0)
                images(sp, image)
                for q in range(2):
                    sp.wait_ge(y_out[q], nb * 16 * (T // 2 + 1 - q) + 16)

            NCONST = 2 + 4 + 4 + 4

            @block.tensor
            def _(pe):
                pe.sem_inc(prod_done, SEED)
                pe.sem_inc(conv_done, SEED)
                pe.sem_inc(out_done, SEED)
                pe.wait_ge(const_in, 16 * NCONST)
                for k in range(4):
                    for h in range(2):
                        mm = nc.tensor.matmul(ps_in[0][:, k * nb:(k + 1) * nb], wcur[:, h, k, :], negmr[:, h, :], start=(h == 0), stop=(h == 1))
                mm.then_inc(bias_mm, 1)
                pe.wait_ge(built, 3)

                def product(b, t, q):
                    pe.wait_ge(xhat_done, b * T + t + (1 + SEED))
                    for k in range(4):
                        for pair in range(2):
                            pe.wait_ge(hat_done, b * (8 * T) + (t * 8 + (2 * k + pair) - 1) + SEED)
                            for h in range(2):
                                mm = nc.tensor.matmul(ps_in[pair][:], wcur[:, h, k, :], xh[q][:, h, 2 * pair:2 * pair + 2, :].rearrange("c f n -> c (f n)"), start=(h == 0), stop=(h == 1))
                            mm.then_inc(prod_done, 1)

                def conv(b, t, q, half, tail=False):
                    if not tail:
                        pe.wait_ge(pa_in[q], b * (SET * T // 2) + (t - q) * (SET // 2) + (SET + 16))
                    pe.wait_ge(edge_done, b * (T + 1) + t + (1 + SEED))
                    rows = 1 if tail else PR
                    for i in range(8 * half, 8 * half + 8):
                        pe.wait_ge(gelu_done, b * CONV + (t * UNITS + i - 1) + SEED)
                        out = ps_cv[i % 2][:, 0:rows * (PC + 1)].rearrange("p (r w) -> p r w", w=PC + 1)
                        last = 1 if tail else 3
                        for n in range(last + 1):
                            dr, dc = n // 2, n % 2
                            mm = nc.tensor.matmul(out[:, :, 1 - dc:PC + 1 - dc], mats[:, n, i, :],
                                                  pa[q][:, i // 4, (i % 4) // 2, dr:dr + rows, :],
                                                  start=(n == 0), stop=(n == last), skip_group_check=True)
                        mm.then_inc(conv_done, 1)

                def project(b, t, q, tail=False):
                    pe.wait_ge(gate_done, b * GATE + (t * 4 + 4) + SEED)
                    pe.wait_ge(y_done, b * OUT + t * 4 + SEED)
                    n = SIDE if tail else 512
                    for m in range(2):
                        for ch in range(1 if tail else 2):
                            for cs in range(4):
                                mm = nc.tensor.matmul(ps_out[2 * m + ch][:, 0:n], wout[:, cs, m * HALF:(m + 1) * HALF], acc[q][:, cs, ch * 512:ch * 512 + n], start=(cs == 0), stop=(cs == 3))
                            mm.then_inc(out_done, 1)

                def image(b, last):
                    def step(t, q):
                        if static(t, T - 1) and not last:
                            pe.wait_ge(weights_set, b + 2)
                        if not (last and static(t, T - 1)):
                            product(b, t + 1, 1 - q)
                        conv(b, t, q, 0)
                        if not static(t, 0):
                            project(b, t - 1, 1 - q)
                        conv(b, t, q, 1)

                    def tail():
                        conv(b, T, 0, 0, tail=True)
                        conv(b, T, 0, 1, tail=True)
                        project(b, T - 1, 1)
                        project(b, T, 0, tail=True)

                    loop_steps(pe, step, tail)

                pe.wait_ge(weights_set, 1)
                product(0, 0, 0)
                images(pe, image)

            @block.scalar
            def _(act):
                act.sem_inc(hat_done, SEED)
                act.sem_inc(edge_done, SEED)
                act.sem_inc(gelu_done, SEED)
                act.sem_inc(first_done, SEED)
                act.wait_ge(built, 3)

                def evacuate(b, t, q):
                    act.wait_ge(pa_in[1 - q], b * (SET * T // 2) + (t + q) * (SET // 2) + 16)
                    for k in range(4):
                        if k >= 2:
                            act.wait_ge(hidden_done, b * (2 * T) + (t * 2 - 2 + (k - 2) + 1) + SEED)
                        for pair in range(2):
                            act.wait_ge(prod_done, b * (8 * T) + (t * 8 + 2 * k + pair + 1) + SEED)
                            for e in range(2):
                                f = 2 * pair + e
                                dst = ha[:, f, k, :] if k < 2 else hf[:, k - 2, f, :]
                                if f == 0:
                                    last = nc.scalar.activation(dst, ps_in[pair][:, e * PATCH:(e + 1) * PATCH], ACT.Identity, bias=bcur[:, k:k + 1], scale=fw4[:, k, f:f + 1])
                                else:
                                    last = nc.scalar.activation(dst, ps_in[pair][:, e * PATCH:(e + 1) * PATCH], ACT.Copy, scale=fw4[:, k, f:f + 1])
                            last.then_inc(hat_done, 1)

                def edge(b, t, q, first=False, tail=False):
                    if first:
                        act.wait_ge(conv_done, b * CONV + SEED)
                        act.wait_ge(taps_done, b * GATE + SEED)
                        nc.scalar.copy(hp[q][:, :, 0:2, :], zero[:].unsqueeze(2).unsqueeze(3).broadcast_to([P, 2, 2, PADW]))
                        nc.scalar.copy(pa[q][:, :, :, 0, :].rearrange("p j c w -> p (j c) w"), zero[:].unsqueeze(2).broadcast_to([P, 8, PC])).then_inc(edge_done, 1)
                        return
                    act.wait_ge(hidden_done, b * (2 * T) + t * 2 + SEED)
                    act.wait_ge(taps_done, b * GATE + (t * 4 - 4) + SEED)
                    act.wait_ge(pa_in[1 - q], b * (SET * T // 2) + (t + q) * (SET // 2) + 16)
                    act.wait_ge(conv_done, b * CONV + (t * UNITS - UNITS) + SEED)
                    nc.scalar.copy(hp[q][:, :, 0:2, :], hp[1 - q][:, :, ROWS:ROWS + 2, :])
                    if tail:
                        nc.scalar.copy(hp[q][:, :, 2, :], zero[:].unsqueeze(2).broadcast_to([P, 2, PADW]))
                    nc.scalar.copy(pa[q][:, :, :, 0, :].rearrange("p j c w -> p (j c) w"), pa[1 - q][:, :, :, PR, :].rearrange("p j c w -> p (j c) w")).then_inc(edge_done, 1)

                def first_taps(b, t, q, some, rows=ROWS):
                    act.wait_ge(edge_done, b * (T + 1) + t + (1 + SEED))
                    if rows == ROWS:
                        act.wait_ge(hidden_done, b * (2 * T) + t * 2 + (2 + SEED))
                    act.wait_ge(out_done, b * OUT + (0 if static(t, 0, 1) else t * 4 - 4) + SEED)
                    for cs in some:
                        nc.scalar.activation(acc[q][:, cs, 0:rows * SIDE].rearrange("p (r w) -> p r w", w=SIDE), hp[q][:, cs // 2, 0:rows, 0:SIDE],
                                             ACT.Copy, scale=dw[:, cs // 2, cs % 2, 0:1]).then_inc(first_done, 1)

                def gelu(b, t, units, tail=False):
                    act.wait_ge(g_in, b * GIN + t * SET + 16)
                    n = PC + 1 if tail else UNIT
                    for i in units:
                        act.wait_ge(conv_done, b * CONV + (t * UNITS + i + 1) + SEED)
                        nc.scalar.activation(gq[:, i // 4, i % 4, 0:n], ps_cv[i % 2][:, 0:n], ACT.Gelu).then_inc(gelu_done, 1)

                def image(b, last):
                    edge(b, 0, 0, first=True)
                    first_taps(b, 0, 0, range(2))

                    def step(t, q):
                        end = static(t, T - 1)
                        if not (last and end):
                            evacuate(b, t + 1, 1 - q)
                        if static(t, 0):
                            first_taps(b, 0, 0, range(2, 4))
                        gelu(b, t, range(8))
                        edge(b, t + 1, 1 - q, tail=end)
                        for cs in range(4):
                            gelu(b, t, range(8 + 2 * cs, 10 + 2 * cs))
                            first_taps(b, t + 1, 1 - q, [cs], rows=1 if end else ROWS)

                    def tail():
                        gelu(b, T, range(UNITS), tail=True)

                    loop_steps(act, step, tail)

                act.wait_ge(weights_set, 1)
                evacuate(0, 0, 0)
                images(act, image)

            @block.vector
            def _(dve):
                for s in (xhat_done, hidden_done, taps_done, gate_done, y_done):
                    dve.sem_inc(s, SEED)
                dve.memset(dw[:], 0.0)
                dve.memset(fw[:], 0.0)
                dve.memset(zero[:], 0.0)
                dve.memset(xr[0][:], 0.0)
                for p in range(2):
                    dve.memset(hp[p][:], 0.0)
                dve.memset(wout[:], 0.0).then_inc(built, 1)
                dve.wait_ge(const_in, 16 * NCONST)
                dve.wait_ge(bias_mm, 1)
                for k in range(4):
                    nc.vector.tensor_scalar(ball[:, k, :], ps_in[0][:, k * nb:(k + 1) * nb], fw[:, k, 0:1], None, ALU.mult)
                nc.vector.tensor_scalar(fw4[:], fw[:], 0.25, None, ALU.mult).then_inc(built, 1)
                added = 0
                for n in range(16):
                    dr, dc, qy, qx = n >> 3, n >> 2 & 1, n >> 1 & 1, n & 1
                    begun = False
                    for r in range(4):
                        ky, kx = 2 * dr + r // 2 - qy, 2 * dc + r % 2 - qx
                        if not (0 <= ky < 3 and 0 <= kx < 3):
                            continue
                        w = dwA[:, :, 3 * ky + kx]
                        if not begun:
                            nc.vector.tensor_scalar(coef[:, n, :], w, sign[:, r:r + 1], None, ALU.mult).then_inc(coefs_set, 1)
                        else:
                            dve.wait_ge(coefs_set, added)
                            nc.vector.scalar_tensor_tensor(out=coef[:, n, :], in0=w, scalar=sign[:, r:r + 1], in1=coef[:, n, :], op0=ALU.mult, op1=ALU.add).then_inc(coefs_set, 1)
                        begun = True
                        added += 1
                dve.wait_ge(coefs_set, added)
                for n in range(16):
                    last = nc.vector.tensor_tensor(mats[:, n // 4, :, (n % 4) * BLK:(n % 4 + 1) * BLK], coef[:, n, :].unsqueeze(2).broadcast_to([P, UNITS, BLK]),
                                                   eye[:].unsqueeze(1).broadcast_to([P, UNITS, BLK]), ALU.mult)
                last.then_inc(built, 1)
                dve.wait_ge(built, 3)

                n_link = [0]

                def mark(ins):
                    n_link[0] += 1
                    return ins.then_inc(link, 1)

                def linked():
                    dve.wait_ge(link, n_link[0])

                def close():
                    dve.sem_inc(closed, 1)
                    linked()
                    dve.sem_clear(link)
                    n_link[0] = 0

                def frequencies(b, t, q):
                    dve.wait_ge(xs_in, b * (16 * T) + t * 16 + 16)
                    v = xs[:].rearrange("c h (r two w) -> c h r two w", two=2, w=SIDE)
                    o = xh[q][:].rearrange("c h (fy fx) n -> c fy fx h n", fx=2)
                    sums = work[0:HALF, :].rearrange("c (h n) -> c h n", h=2)
                    u = sums.rearrange("c h (n two) -> c h n two", two=2)
                    if not static(t, 0, 1):
                        dve.wait_ge(prod_done, b * (8 * T) + (t * 8 - 8) + SEED)
                    for fy, op in ((0, ALU.add), (1, ALU.subtract)):
                        mark(nc.vector.tensor_tensor(sums.rearrange("c h (r w) -> c h r w", w=SIDE), v[:, :, :, 0, :], v[:, :, :, 1, :], op))
                        linked()
                        nc.vector.tensor_tensor(o[:, fy, 0], u[:, :, :, 0], u[:, :, :, 1], ALU.add)
                        last = nc.vector.tensor_tensor(o[:, fy, 1], u[:, :, :, 0], u[:, :, :, 1], ALU.subtract)
                        if fy == 0:
                            mark(last)
                            linked()
                    last.then_inc(xhat_done, 1)
                    dve.wait_ge(xhat_done, b * T + t + (1 + SEED))

                def hidden(b, t, q, c):
                    dve.wait_ge(hat_done, b * (8 * T) + (t * 8 + 2 * (c + 2) + 2) + SEED)
                    ht = work[:].rearrange("p (f n) -> p f n", f=4)
                    lo, hi = hf[:, c, 0:2, :], hf[:, c, 2:4, :]
                    nc.vector.tensor_tensor(ht[:, 0:2, :], lo, hi, ALU.add)
                    mark(nc.vector.tensor_tensor(ht[:, 2:4, :], lo, hi, ALU.subtract))
                    linked()
                    if c == 0:
                        dve.wait_ge(edge_done, b * (T + 1) + t + SEED)
                    u = ht.rearrange("p (py fx) (r n) -> p py fx r n", fx=2, n=PC)
                    o = hp[q][:, c, 2:ROWS + 2, 1:SIDE + 1].rearrange("p (r py) (n px) -> p py px r n", py=2, px=2)
                    nc.vector.tensor_tensor(o[:, :, 0], u[:, :, 0], u[:, :, 1], ALU.add)
                    nc.vector.tensor_tensor(o[:, :, 1], u[:, :, 0], u[:, :, 1], ALU.subtract).then_inc(hidden_done, 1)
                    dve.wait_ge(hidden_done, b * (2 * T) + (t * 2 + c + 1) + SEED)

                def taps(b, t, q, c, rows=ROWS):
                    made = [0, 0]
                    for tap in range(1, TAPS):
                        h = hp[q][:, c, tap // 3:tap // 3 + rows, tap % 3:tap % 3 + SIDE]
                        for s in range(2):
                            cs = 2 * c + s
                            if tap == 1:
                                dve.wait_ge(first_done, b * GATE + (t * 4 + cs + 1) + SEED)
                            else:
                                dve.wait_ge(link, made[s])
                            out = acc[q][:, cs, 0:rows * SIDE].rearrange("p (r w) -> p r w", w=SIDE)
                            ins = nc.vector.scalar_tensor_tensor(out=out, in0=h, scalar=dw[:, c, s, tap:tap + 1], in1=out, op0=ALU.mult, op1=ALU.add)
                            if tap < TAPS - 1:
                                mark(ins)
                                made[s] = n_link[0]
                            else:
                                ins.then_inc(taps_done, 1)

                def gates(b, t, q, tail=False):
                    dve.wait_ge(taps_done, b * GATE + t * 4 + (4 + SEED))
                    dve.wait_ge(g_in, b * GIN + t * SET + ((SET // 2 if tail else SET) + 16))
                    for cs in range(4):
                        for qx in range(2):
                            lo = 1 - qx
                            if tail:
                                d = acc[q][:, cs, 0:SIDE].rearrange("p (w two) -> p w two", two=2)[:, :, lo]
                                s = g[:, qx, cs, lo:lo + PC]
                            else:
                                d = acc[q][:, cs, :].rearrange("p (r qy w two) -> p qy r w two", qy=2, w=PC, two=2)[:, :, :, :, lo]
                                s = g[:, qx:4:2, cs, :].rearrange("p qy (r w) -> p qy r w", w=PC + 1)[:, :, :, lo:lo + PC]
                            last = nc.vector.tensor_tensor(d, s, d, ALU.mult)
                        last.then_inc(gate_done, 1)

                def residual(b, t, q, tail=False, first=False):
                    n = SIDE if tail else 512
                    dve.wait_ge(xr_in[q], b * (16 * (T // 2 + 1 - q)) + (t - q) * 8 + 16)
                    parts = [(m, ch) for m in range(2) for ch in range(1 if tail else 2)]
                    summed = []

                    def records(i):
                        m, ch = parts[i]
                        lo = SIDE if (first and ch == 0) else 0
                        dve.wait_ge(link, summed[i])
                        nc.vector.bn_stats(stats[:, m, bass.ds((t * 2 + ch) * 6, 6)],
                                           xr[q][:, m, ch * 512 + lo:ch * 512 + n]).then_inc(y_done, 1)

                    for i, (m, ch) in enumerate(parts):
                        dve.wait_ge(out_done, b * OUT + (t * 4 + i + 1) + SEED)
                        s = slice(ch * 512, ch * 512 + n)
                        mark(nc.vector.tensor_tensor(xr[q][:, m, s], ps_out[2 * m + ch][:, 0:n], xr[q][:, m, s], ALU.add))
                        summed.append(n_link[0])
                        if i:
                            records(i - 1)
                    records(len(parts) - 1)

                def set_weights(b):
                    dve.wait_ge(w_loaded, b * 16 + 16)
                    dve.wait_ge(hat_done, b * (8 * T) + SEED)
                    for h in range(2):
                        nc.vector.tensor_scalar(wcur[:, h], wcur[:, h], rstd[:, h, bass.ds(b, 1)], None, ALU.mult)
                    nc.vector.tensor_copy(bcur[:], ball[:, :, bass.ds(b, 1)].rearrange("p k o -> p (k o)")).then_inc(weights_set, 1)

                def image(b, last):
                    for c in range(2):
                        hidden(b, 0, 0, c)
                    close()

                    def step(t, q):
                        if not static(t, 0):
                            gates(b, t - 1, 1 - q)
                        if not (last and static(t, T - 2, T - 1)):
                            frequencies(b, t + 2, q)
                        if static(t, 0):
                            taps(b, t, q, 0)
                        if not static(t, T - 1):
                            for c in range(2):
                                hidden(b, t + 1, 1 - q, c)
                        for c in range(1 if static(t, 0) else 0, 2):
                            taps(b, t, q, c)
                            if c == 0 and static(t, T - 2) and not last:
                                set_weights(b + 1)
                        if not static(t, 0):
                            residual(b, t - 1, 1 - q, first=static(t, 1))
                        close()

                    def tail():
                        gates(b, T - 1, 1)
                        for c in range(2):
                            taps(b, T, 0, c, rows=1)
                        residual(b, T - 1, 1)
                        gates(b, T, 0, tail=True)
                        residual(b, T, 0, tail=True)
                        dve.wait_ge(y_done, b * OUT + (OUT + SEED))
                        dve.sem_inc(closed, 1)
                        for h in range(2):
                            last = nc.vector.bn_aggr(pair[:, h], stats[:, h])
                        last.then_inc(paired, 1)
                        dve.wait_ge(paired, b + 1)
                        nc.vector.tensor_copy(agg[:, :, bass.ds(b, 1), :].rearrange("c h o t -> c h (o t)"), pair[:]).then_inc(kept, 1)
                        dve.wait_ge(kept, b + 1)
                        close()

                    loop_steps(dve, step, tail)

                set_weights(0)
                frequencies(0, 0, 0)
                frequencies(0, 1, 1)
                close()
                images(dve, image)


def layer1_in(nc, y, w1T, w1x0, w0T, b0, rstd, negmr, x1, cat, nb):
    rows = 16
    px = rows * SIDE
    per = SIDE // rows
    C1 = w1T.shape[1]
    C0 = C1 // 3
    with ExitStack() as ctx:
        def sb(name, shape):
            return ctx.enter_context(nc.sbuf_tensor(name, shape, F32))

        def sem(name):
            return ctx.enter_context(nc.semaphore(name))

        w1 = sb("w1", [HALF, 2, C1])
        w1cur = sb("w1cur", [HALF, 2, C1])
        wx = sb("wx", [C0, 2, HALF])
        w0 = sb("w0", [C0, C0])
        b0s = sb("b0s", [C1, 1])
        ball = sb("b1all", [C1, nb])
        bcur = sb("b1cur", [C1, 1])
        yin = [sb(f"yin{p}", [HALF, 2, px]) for p in range(2)]
        z = [sb(f"z{p}", [C1, px]) for p in range(2)]
        ps = [ctx.enter_context(nc.psum_tensor(f"ps_1{i}", [C1, 512], F32)) for i in range(4)]
        ps_w = ctx.enter_context(nc.psum_tensor("ps_w", [HALF, 2 * C0], F32))
        const_in = sem("in_const")
        composed = sem("in_composed")
        bias_mm = sem("in_bias_mm")
        weights_set = sem("in_weights")
        pe_turn = sem("in_pe_turn")
        loaded = [sem(f"in_loaded{p}") for p in range(2)]
        stored = [sem(f"in_stored{p}") for p in range(2)]
        stored0 = [sem(f"in_stored0{p}") for p in range(2)]
        mm1 = sem("in_mm1")
        z_done = sem("in_z")
        yv = y.rearrange("b (h c) r w -> c b h (r w)", h=2)
        x1v = x1.rearrange("b c r w -> c b (r w)")
        catv = cat.rearrange("b c r w -> c b (r w)")

        with nc.Block() as block:
            @block.sync
            def _(sp):
                for q in range(2):
                    sp.sem_inc(stored[q], 16)
                    sp.sem_inc(stored0[q], 16)
                sp.dma_start(w1[:], w1T.rearrange("(h c) o -> c h o", h=2)).then_inc(const_in, 16)
                sp.dma_start(wx[:], w1x0).then_inc(const_in, 16)
                sp.dma_start(w0[:], w0T).then_inc(const_in, 16)
                sp.dma_start(b0s[:], b0).then_inc(const_in, 16)
                with sp.Fori(0, nb) as b:
                    with sp.Fori(0, per // 2) as i:
                        for q in range(2):
                            sp.wait_ge(mm1, b * (4 * per) + (i * 8 + 4 * q - 4) + SEED)
                            sp.dma_start(yin[q][:], yv[:, b, :, bass.ds((i * 2 + q) * px, px)]).then_inc(loaded[q], 16)

            @block.tensor
            def _(pe):
                pe.sem_inc(mm1, SEED)
                pe.wait_ge(const_in, 64)
                for h in range(2):
                    mm = nc.tensor.matmul(ps_w[:, h * C0:(h + 1) * C0], wx[:, h, :], w0[:], start=True, stop=True)
                mm.then_inc(composed, 1)
                pe.wait_ge(weights_set, 1)
                for h in range(2):
                    mm = nc.tensor.matmul(ps[0][:, 0:nb], w1[:, h, :], negmr[:, h, :], start=(h == 0), stop=(h == 1))
                mm.then_inc(bias_mm, 1)
                with pe.Fori(0, nb) as b:
                    pe.wait_ge(weights_set, b + 3)
                    pe.sem_inc(pe_turn, 1)
                    with pe.Fori(0, per // 2) as i:
                        for q in range(2):
                            pe.wait_ge(loaded[q], b * (8 * per) + i * 16 + 16)
                            for c in range(4):
                                pe.wait_ge(z_done, b * (4 * per) + (i * 8 + 4 * q + c - 3) + SEED)
                                for h in range(2):
                                    mm = nc.tensor.matmul(ps[c][:], w1cur[:, h, :], yin[q][:, h, c * 512:(c + 1) * 512], start=(h == 0), stop=(h == 1))
                                mm.then_inc(mm1, 1)

            @block.scalar
            def _(act):
                act.sem_inc(z_done, SEED)
                with act.Fori(0, nb) as b:
                    act.wait_ge(weights_set, b + 3)
                    with act.Fori(0, per // 2) as i:
                        for q in range(2):
                            act.wait_ge(stored[q], b * (8 * per) + i * 16 + 16)
                            act.wait_ge(stored0[q], b * (8 * per) + i * 16 + 16)
                            for c in range(4):
                                act.wait_ge(mm1, b * (4 * per) + (i * 8 + 4 * q + c + 1) + SEED)
                                nc.scalar.activation(z[q][:, c * 512:(c + 1) * 512], ps[c][:], ACT.Identity, bias=bcur[:, 0:1]).then_inc(z_done, 1)
                            act.wait_ge(z_done, b * (4 * per) + (i * 8 + 4 * q + 4) + SEED)
                            act.dma_start(x1v[C0:C1, b, bass.ds((i * 2 + q) * px, px)], z[q][C0:C1, :]).then_inc(stored[q], 16)
                            act.dma_start(catv[0:C0, b, bass.ds((i * 2 + q) * px, px)], z[q][0:C0, :]).then_inc(stored0[q], 16)
                for q in range(2):
                    act.wait_ge(stored[q], nb * 8 * per + 16)
                    act.wait_ge(stored0[q], nb * 8 * per + 16)

            @block.vector
            def _(dve):
                dve.wait_ge(composed, 1)
                nc.vector.tensor_copy(w1[:, :, 0:C0], ps_w[:].rearrange("c (h o) -> c h o", h=2)).then_inc(weights_set, 1)
                dve.wait_ge(bias_mm, 1)
                dve.wait_ge(const_in, 64)
                nc.vector.tensor_scalar(ball[:], ps[0][:, 0:nb], b0s[:, 0:1], None, ALU.add).then_inc(weights_set, 1)
                dve.wait_ge(weights_set, 2)
                with dve.Fori(0, nb) as b:
                    dve.wait_ge(mm1, b * (4 * per) + SEED)
                    dve.wait_ge(z_done, b * (4 * per) + SEED)
                    for h in range(2):
                        nc.vector.tensor_scalar(w1cur[:, h], w1[:, h], rstd[:, h, bass.ds(b, 1)], None, ALU.mult)
                    nc.vector.tensor_copy(bcur[:], ball[:, bass.ds(b, 1)]).then_inc(weights_set, 1)


def layer1_out(nc, y, cat, w2T, out, nb):
    rows = 16
    px = rows * SIDE
    per = SIDE // rows
    C1 = cat.shape[1]
    K = w2T.shape[0]
    with ExitStack() as ctx:
        def sb(name, shape):
            return ctx.enter_context(nc.sbuf_tensor(name, shape, F32))

        def sem(name):
            return ctx.enter_context(nc.semaphore(name))

        w2 = sb("w2", [K, 2 * HALF])
        yin = [sb(f"oy{p}", [HALF, 2, px]) for p in range(2)]
        cin = [sb(f"oc{p}", [K, px]) for p in range(2)]
        oo = [sb(f"oo{p}", [HALF, 2, px]) for p in range(2)]
        ps = [ctx.enter_context(nc.psum_tensor(f"ps_o{i}", [HALF, 512], F32)) for i in range(8)]
        const_in = sem("out_const")
        zeroed = sem("out_zeroed")
        y_in = [sem(f"out_y{p}") for p in range(2)]
        c_in = [sem(f"out_c{p}") for p in range(2)]
        stored = [sem(f"out_stored{p}") for p in range(2)]
        mm = sem("out_mm")
        summed = sem("out_sum")
        yv = y.rearrange("b (h c) r w -> c b h (r w)", h=2)
        ov = out.rearrange("b (h c) r w -> c b h (r w)", h=2)
        catv = cat.rearrange("b c r w -> c b (r w)")

        with nc.Block() as block:
            @block.sync
            def _(sp):
                sp.dma_start(w2[:], w2T).then_inc(const_in, 16)
                sp.wait_ge(zeroed, 1)
                with sp.Fori(0, nb) as b:
                    with sp.Fori(0, per // 2) as i:
                        for q in range(2):
                            sp.wait_ge(summed, b * (8 * per) + (i * 16 + 8 * q - 8) + SEED)
                            sp.dma_start(cin[q][0:C1], catv[:, b, bass.ds((i * 2 + q) * px, px)]).then_inc(c_in[q], 16)
                            sp.dma_start(yin[q][:], yv[:, b, :, bass.ds((i * 2 + q) * px, px)]).then_inc(y_in[q], 16)

            @block.tensor
            def _(pe):
                pe.wait_ge(const_in, 16)
                with pe.Fori(0, nb) as b:
                    with pe.Fori(0, per // 2) as i:
                        for q in range(2):
                            pe.wait_ge(c_in[q], b * (8 * per) + i * 16 + 16)
                            for m in range(2):
                                for c in range(4):
                                    pe.wait_ge(summed, b * (8 * per) + (i * 16 + 8 * q + 4 * m + c - 7) + SEED)
                                    nc.tensor.matmul(ps[4 * m + c][:], w2[:, m * HALF:(m + 1) * HALF], cin[q][:, c * 512:(c + 1) * 512], start=True, stop=True).then_inc(mm, 1)

            @block.vector
            def _(dve):
                dve.sem_inc(summed, SEED)
                for q in range(2):
                    ins = dve.memset(cin[q][:], 0.0)
                ins.then_inc(zeroed, 1)
                with dve.Fori(0, nb) as b:
                    with dve.Fori(0, per // 2) as i:
                        for q in range(2):
                            dve.wait_ge(y_in[q], b * (8 * per) + i * 16 + 16)
                            dve.wait_ge(stored[q], b * (8 * per) + i * 16 + 16)
                            for m in range(2):
                                for c in range(4):
                                    dve.wait_ge(mm, b * (8 * per) + (i * 16 + 8 * q + 4 * m + c + 1))
                                    s = slice(c * 512, (c + 1) * 512)
                                    nc.vector.tensor_tensor(oo[q][:, m, s], ps[4 * m + c][:], yin[q][:, m, s], ALU.add).then_inc(summed, 1)

            @block.scalar
            def _(act):
                for q in range(2):
                    act.sem_inc(stored[q], 16)
                with act.Fori(0, nb) as b:
                    with act.Fori(0, per // 2) as i:
                        for q in range(2):
                            act.wait_ge(summed, b * (8 * per) + (i * 16 + 8 * q + 8) + SEED)
                            act.dma_start(ov[:, b, :, bass.ds((i * 2 + q) * px, px)], oo[q][:]).then_inc(stored[q], 16)
                for q in range(2):
                    act.wait_ge(stored[q], nb * 8 * per + 16)


FRAC = 16 * SIDE
HALFW = SIDE // 2 + 1
FOUR = 16 * HALFW
ALL = FRAC + FOUR
PI = float(np.pi)
TWO_PI = 2 * PI
PI_A = 6.28125
PI_B = float(np.float32(np.round((TWO_PI - PI_A) * 2**22) / 2**22))
PI_C = TWO_PI - PI_A - PI_B
ROUND = 1.5 * 2.0**23
PI_MAX = 3.1415925
TINY = 1e-30


def layer1_planes(nc, x1, cat, consts, mixes, biases, mask, scratch, nb):
    polar1, polar2, back1, back2 = scratch
    GROUPS = 24
    with ExitStack() as ctx:
        def sb(name, shape):
            return ctx.enter_context(nc.sbuf_tensor(name, shape, F32))

        def sem(name):
            return ctx.enter_context(nc.semaphore(name))

        c_frac, c_ifrac, c_f1, c_f2, c_i1, c_i2 = consts
        frac = sb("frac", [P, 2, 2 * SIDE])
        ifrac = sb("ifrac", [P, 2, 2 * SIDE])
        four1 = sb("four1", [P, 2 * SIDE])
        four2 = sb("four2", [P, 2, 2 * HALFW])
        inv1 = sb("inv1", [P, 2, 2 * SIDE])
        inv2 = sb("inv2", [HALFW, 2, SIDE])
        mix = sb("mix", [P, 13, P])
        bias = sb("bias", [P, 5])
        msk = sb("msk", [P, 18, SIDE])
        xp = sb("xp", [P, 32, SIDE])
        tb = [sb(f"tb{q}", [P, 2 * SIDE]) for q in range(2)]
        sq = [sb(f"sq{q}", [P, 2 * SIDE]) for q in range(2)]
        ri = sb("ri", [P, 2, ALL])
        t = sb("t", [P, 4, ALL])
        gm = sb("gm", [P, 2, ALL])
        mp = sb("mp", [P, 18, PADW])
        mo = sb("mo", [P, 2, ALL])
        z = sb("z", [P, 2, ALL])
        po = gm[:].rearrange("p k n -> p (k n)")[:, 0:32 * SIDE].rearrange("p (c w) -> p c w", w=SIDE)
        ps_a = [ctx.enter_context(nc.psum_tensor(f"ps_a{q}", [P, 512], F32)) for q in range(2)]
        ps_b = [ctx.enter_context(nc.psum_tensor(f"ps_b{q}", [P, 512], F32)) for q in range(2)]
        ps_c = [ctx.enter_context(nc.psum_tensor(f"ps_c{q}", [P, 512], F32)) for q in range(4)]

        const_in = sem("pl_const")
        zeroed = sem("pl_zeroed")
        xp_in = sem("xp_in")
        polar_out = sem("polar_out")
        gm_in = sem("gm_in")
        back_out = sem("back_out")
        z_in = sem("z_in")
        cat_out = sem("cat_out")
        pass1 = sem("pass1")
        between = sem("between")
        pass2 = sem("pass2")
        taken = sem("taken")
        squared = sem("squared")
        pol_a = sem("pol_a")
        pol_v = sem("pol_v")
        inv_v = sem("inv_v")
        inv_a = sem("inv_a")
        mix_mm = sem("mix_mm")
        mix_ev = sem("mix_ev")
        mix_v = sem("mix_v")
        ang_v = sem("ang_v")
        ang_a = sem("ang_a")
        turn = sem("pl_turn")
        link = sem("pl_link")
        closed = sem("pl_closed")

        def turns(forward, mixed, inverse, angles, eng):
            forward(0, 0, None)
            angles(None, 0)
            forward(1, 32, None)
            mixed(0, 1)
            inverse(None, 0, 1)
            with eng.Fori(1, nb - 1) as i:
                forward(i + 1, i * 64, i - 1)
                mixed(i, i + 1)
                inverse(i - 1, i * 64 + 32, i + 1)
            angles(nb - 2, None)
            mixed(nb - 1, None)
            inverse(nb - 2, (nb - 1) * 64, None)
            angles(nb - 1, None)
            inverse(nb - 1, (nb - 1) * 64 + 32, None)

        by_row = "c h w -> h c w"
        by_block = "c (k r) w -> k c (r w)"

        with nc.Block() as block:
            @block.sync
            def _(sp):
                for s in (polar_out, back_out, cat_out, gm_in, z_in):
                    sp.sem_inc(s, 16)
                for dst, src in ((frac, c_frac), (ifrac, c_ifrac), (four1, c_f1), (four2, c_f2), (inv1, c_i1), (inv2, c_i2), (mix, mixes), (bias, biases), (msk, mask)):
                    sp.dma_start(dst[:], src).then_inc(const_in, 16)
                sp.wait_ge(zeroed, 1)

                def load_planes(i):
                    if not (isinstance(i, int) and i == 0):
                        sp.wait_ge(pass1, (i * 32 if isinstance(i, int) else i * 64 - 96) + SEED)
                        sp.sem_inc(turn, 1)
                    for c in range(0, 32, 8):
                        sp.dma_start(xp[:, c:c + 8, :], x1[i].rearrange(by_row)[:, 16 + c:24 + c]).then_inc(xp_in, 16)

                def store_polar(i):
                    sp.wait_ge(pol_a, i * 4 + (4 + SEED))
                    sp.sem_inc(turn, 1)
                    sp.wait_ge(gm_in, i * 96 + 16)
                    sp.sem_inc(turn, 1)
                    for k in range(2):
                        sp.dma_start(polar1[k].rearrange(by_row), t[:, k, 0:FRAC].rearrange("h (c w) -> h c w", w=SIDE)).then_inc(polar_out, 16)
                        sp.dma_start(polar2[k].rearrange(by_row), t[:, k, FRAC:ALL].rearrange("h (c w) -> h c w", w=HALFW)).then_inc(polar_out, 16)

                def load_mix(i):
                    sp.wait_ge(polar_out, i * 64 + (64 + 16))
                    sp.sem_inc(turn, 1)
                    if not (isinstance(i, int) and i == 0):
                        sp.wait_ge(mix_mm, i * GROUPS + SEED)
                        sp.sem_inc(turn, 1)
                        sp.wait_ge(cat_out, i * 16)
                        sp.sem_inc(turn, 1)
                    for k in range(2):
                        sp.dma_start(gm[:, k, 0:FRAC], polar1[k].rearrange(by_block, k=8)).then_inc(gm_in, 16)
                        sp.dma_start(gm[:, k, FRAC:ALL], polar2[k].rearrange(by_block, k=8)).then_inc(gm_in, 16)
                    rows = polar1[0].rearrange("c (k r) w -> k c r w", k=8)
                    sp.dma_start(mp[16:P, 0, 1:SIDE + 1], rows[0:7, :, 15, :]).then_inc(gm_in, 16)
                    sp.dma_start(mp[0:P - 16, 17, 1:SIDE + 1], rows[1:8, :, 0, :]).then_inc(gm_in, 16)

                def store_cat(i):
                    sp.wait_ge(inv_a, i + (1 + SEED))
                    sp.sem_inc(turn, 1)
                    sp.dma_start(cat[i].rearrange(by_row)[:, 16:48], po).then_inc(cat_out, 16)

                def regroup(i):
                    sp.wait_ge(ang_v, i * 2 + (2 + SEED))
                    sp.sem_inc(turn, 1)
                    sp.wait_ge(z_in, i * 96 + 16)
                    sp.sem_inc(turn, 1)
                    for k, back in enumerate((back1, back2)):
                        for c in range(2):
                            src = z[:, c, 0:FRAC] if k == 0 else z[:, c, FRAC:ALL]
                            sp.dma_start(back[c].rearrange(by_block, k=8), src).then_inc(back_out, 16)
                    sp.wait_ge(back_out, i * 64 + (64 + 16))
                    sp.sem_inc(turn, 1)
                    for k in range(2):
                        for c in (0, 8):
                            sp.dma_start(z[:, k, c * SIDE:(c + 8) * SIDE].rearrange("h (c w) -> h c w", w=SIDE), back1[k].rearrange(by_row)[:, c:c + 8]).then_inc(z_in, 16)
                        sp.dma_start(z[:, k, FRAC:ALL].rearrange("h (c w) -> h c w", w=HALFW), back2[k].rearrange(by_row)).then_inc(z_in, 16)

                load_planes(0)
                load_planes(1)
                store_polar(0)
                load_mix(0)
                load_planes(2)
                store_polar(1)
                with sp.Fori(1, nb - 2) as i:
                    load_mix(i)
                    regroup(i - 1)
                    load_planes(i + 2)
                    store_polar(i + 1)
                    store_cat(i - 1)
                load_mix(nb - 2)
                regroup(nb - 3)
                store_polar(nb - 1)
                store_cat(nb - 3)
                load_mix(nb - 1)
                regroup(nb - 2)
                store_cat(nb - 2)
                regroup(nb - 1)
                store_cat(nb - 1)
                sp.wait_ge(cat_out, nb * 16 + 16)

            @block.tensor
            def _(pe):
                for s in (pass1, pass2, mix_mm):
                    pe.sem_inc(s, SEED)
                pe.wait_ge(const_in, 16 * 9)

                def transform(base, first, second):
                    for n in range(33):
                        if n < 32:
                            pe.wait_ge(between, base + (n - 1 + SEED))
                            first(n, ps_a[n % 2]).then_inc(pass1, 1)
                        if n > 0:
                            c = n - 1
                            pe.wait_ge(between, base + (c + 1 + SEED))
                            pe.wait_ge(taken, base + (c - 1 + SEED))
                            second(c, ps_b[c % 2]).then_inc(pass2, 1)

                def forward(i, base, late):
                    pe.wait_ge(xp_in, i * 64 + 64)

                    def first(c, out):
                        return nc.tensor.matmul(out[:, 0:256], xp[:, c, :], frac[:, 0, :] if c < 16 else four1[:], start=True, stop=True)

                    def second(c, out):
                        w = frac if c < 16 else four2
                        n = w.shape[2]
                        for k in range(2):
                            mm = nc.tensor.matmul(out[:, 0:n], tb[c % 2][:, k * SIDE:(k + 1) * SIDE], w[:, k, :], start=(k == 0), stop=(k == 1))
                        return mm

                    transform(base, first, second)

                def inverse(i, base, early):
                    if i is None:
                        return
                    pe.wait_ge(z_in, i * 96 + (96 + 16))

                    def first(c, out):
                        n, at, w = (SIDE, c * SIDE, ifrac) if c < 16 else (HALFW, FRAC + (c - 16) * HALFW, inv1)
                        for k in range(2):
                            mm = nc.tensor.matmul(out[0:n, 0:256], z[:, k, at:at + n], w[:, k, :], start=(k == 0), stop=(k == 1))
                        return mm

                    def second(c, out):
                        n, w, m = (P, ifrac, 256) if c < 16 else (HALFW, inv2, SIDE)
                        for k in range(2):
                            mm = nc.tensor.matmul(out[:, 0:m], tb[c % 2][0:n, k * SIDE:(k + 1) * SIDE], w[:, k, :], start=(k == 0), stop=(k == 1))
                        return mm

                    transform(base, first, second)

                def mixed(i, early):
                    pe.wait_ge(gm_in, i * 96 + (96 + 16))
                    q4 = FOUR // 4

                    def group(n, products):
                        pe.wait_ge(mix_ev, i * GROUPS + (n - 3 + SEED))
                        for k, (w, src) in enumerate(products):
                            shape = src.shape
                            cols = int(np.prod(shape[1:]))
                            mm = nc.tensor.matmul(ps_c[n % 4][:, 0:cols], mix[:, w, :], src, start=(k == 0), stop=(k == len(products) - 1))
                        mm.then_inc(mix_mm, 1)

                    for j in range(4):
                        group(j, [(11, gm[:, 1, j * 512:(j + 1) * 512])])
                    for j in range(4):
                        group(4 + j, [(12, gm[:, 1, FRAC + j * q4:FRAC + (j + 1) * q4])])
                    for j in range(4):
                        group(8 + j, [(12, gm[:, 0, FRAC + j * q4:FRAC + (j + 1) * q4])])
                    for j in range(4):
                        group(12 + j, [(9, gm[:, 0, j * 512:(j + 1) * 512])])
                    pe.wait_ge(mix_v, i * 5 + (1 + SEED))
                    for j in range(4):
                        group(16 + j, [(tap, mp[:, 4 * j + tap // 3:4 * j + tap // 3 + 4, tap % 3:tap % 3 + SIDE]) for tap in range(9)])
                    for j in range(4):
                        pe.wait_ge(mix_v, i * 5 + (2 + j + SEED))
                        group(20 + j, [(10, gm[:, 0, j * 512:(j + 1) * 512])])

                turns(forward, mixed, inverse, lambda late, early: None, pe)

            @block.scalar
            def _(act):
                for s in (between, squared, pol_a, inv_a, mix_ev, ang_a):
                    act.sem_inc(s, SEED)
                act.wait_ge(const_in, 16 * 9)

                def copy_between(base, rows, then):
                    for n in range(32):
                        act.wait_ge(pass1, base + (n + 1 + SEED))
                        act.wait_ge(pass2, base + (n - 1 + SEED))
                        m = rows(n)
                        nc.scalar.copy(tb[n % 2][0:m], ps_a[n % 2][0:m, 0:256]).then_inc(between, 1)
                        if n > 0:
                            then(n - 1)
                    then(31)

                def absolutes(i):
                    act.wait_ge(polar_out, i * 64 + 16)
                    nc.scalar.activation(t[:, 0, :], ri[:, 0, :], ACT.Abs)
                    nc.scalar.activation(t[:, 1, :], ri[:, 1, :], ACT.Abs).then_inc(pol_a, 1)

                def arctan(i):
                    act.wait_ge(pol_v, i * 3 + (1 + SEED))
                    nc.scalar.activation(t[:, 1, :], t[:, 3, :], ACT.Arctan).then_inc(pol_a, 1)

                def square(i, k):
                    act.wait_ge(pol_v, i * 3 + (2 + SEED))
                    ins = nc.scalar.activation(ri[:, k, :], ri[:, k, :], ACT.Square)
                    if k == 1:
                        ins.then_inc(pol_a, 1)

                def root(i):
                    act.wait_ge(pol_v, i * 3 + (3 + SEED))
                    nc.scalar.activation(t[:, 0, :], t[:, 0, :], ACT.Sqrt).then_inc(pol_a, 1)

                def cosine(i):
                    act.wait_ge(ang_v, i * 2 + (1 + SEED))
                    nc.scalar.activation(z[:, 0, :], z[:, 0, :], ACT.Sin).then_inc(ang_a, 1)

                def sine(i):
                    nc.scalar.activation(mo[:, 1, :], mo[:, 1, :], ACT.Sin).then_inc(ang_a, 1)

                def forward(i, base, late):
                    def then(c):
                        if late is not None and c == 22:
                            cosine(late)
                        if late is not None and c == 25:
                            sine(late)

                    copy_between(base, lambda n: P, then)
                    act.wait_ge(taken, base + (32 + SEED))
                    absolutes(i)

                def angles(late, early):
                    if late is not None:
                        cosine(late)
                        sine(late)
                    if early is not None:
                        arctan(early)
                        square(early, 0)
                        square(early, 1)
                        root(early)

                def inverse(i, base, early):
                    if i is None:
                        for k in range(2):
                            square(early, k)
                        root(early)
                        return

                    def then(c):
                        if c < 16:
                            act.wait_ge(pass2, base + (c + 1 + SEED))
                            act.wait_ge(taken, base + (c - 1 + SEED))
                            nc.scalar.activation(sq[c % 2][:], ps_b[c % 2][:, 0:256], ACT.Square).then_inc(squared, 1)
                        if early is not None:
                            if c in (19, 21):
                                square(early, (c - 19) // 2)
                            if c == 27:
                                root(early)

                    copy_between(base, lambda n: P if n < 16 else HALFW, then)
                    act.wait_ge(inv_v, i + (1 + SEED))
                    nc.scalar.activation(po[:, 0:16, :], po[:, 0:16, :], ACT.Sqrt).then_inc(inv_a, 1)

                def mixed(i, early):
                    act.wait_ge(ang_v, i * 2 + SEED)
                    q4 = FOUR // 4

                    def take(n, dst, k):
                        act.wait_ge(mix_mm, i * GROUPS + (n + 1 + SEED))
                        m = dst.shape[1]
                        nc.scalar.activation(dst, ps_c[n % 4][:, 0:m], ACT.Identity, bias=bias[:, k:k + 1]).then_inc(mix_ev, 1)

                    for j in range(4):
                        take(j, mo[:, 1, j * 512:(j + 1) * 512], 3)
                    for k in range(2):
                        for j in range(4):
                            take(4 + 4 * k + j, mo[:, 1 - k, FRAC + j * q4:FRAC + (j + 1) * q4], 4)
                    act.wait_ge(mix_v, i * 5 + (1 + SEED))
                    for j in range(4):
                        take(12 + j, gm[:, 0, j * 512:(j + 1) * 512], 1)
                    for j in range(4):
                        take(16 + j, gm[:, 1, j * 512:(j + 1) * 512], 0)
                        if j == 2 and early is not None:
                            arctan(early)
                    for j in range(4):
                        take(20 + j, mo[:, 0, j * 512:(j + 1) * 512], 2)

                turns(forward, mixed, inverse, angles, act)

            @block.vector
            def _(dve):
                for s in (taken, pol_v, inv_v, mix_v, ang_v):
                    dve.sem_inc(s, SEED)
                dve.memset(mp[:], 0.0).then_inc(zeroed, 1)
                dve.wait_ge(zeroed, 1)
                v = nc.vector
                n_link = [0]

                def mark(ins):
                    n_link[0] += 1
                    ins.then_inc(link, 1)

                def linked():
                    dve.wait_ge(link, n_link[0])

                def close():
                    dve.sem_inc(closed, 1)
                    linked()
                    dve.sem_clear(link)
                    n_link[0] = 0

                def polar(i, n):
                    re, im = ri[:, 0, :], ri[:, 1, :]
                    t0, t1, t2, t3 = (t[:, k, :] for k in range(4))
                    linked()
                    if n == 0:
                        dve.wait_ge(pol_a, i * 4 + (1 + SEED))
                        mark(v.tensor_tensor(t2, t0, t1, ALU.max))
                    elif n == 1:
                        mark(v.tensor_tensor(t3, t0, t1, ALU.min))
                    elif n == 2:
                        mark(v.tensor_tensor(t0, t1, t0, ALU.is_gt))
                    elif n == 3:
                        mark(v.tensor_scalar(t2, t2, TINY, None, ALU.max))
                    elif n < 8:
                        w = ALL // 4
                        part = t[:, 2, (n - 4) * w:(n - 3) * w]
                        mark(v.reciprocal(part, part))
                    elif n == 8:
                        v.tensor_tensor(t3, t3, t2, ALU.mult).then_inc(pol_v, 1)
                    elif n == 9:
                        dve.wait_ge(pol_a, i * 4 + (2 + SEED))
                        dve.wait_ge(pol_v, i * 3 + (1 + SEED))
                        mark(v.tensor_scalar(t2, t1, -2.0, PI / 2, ALU.mult, ALU.add))
                    elif n == 10:
                        mark(v.tensor_tensor(t2, t2, t0, ALU.mult))
                    elif n == 11:
                        mark(v.tensor_tensor(t1, t1, t2, ALU.add))
                    elif n == 12:
                        mark(v.tensor_scalar(t2, t1, -2.0, PI, ALU.mult, ALU.add))
                    elif n == 13:
                        mark(v.scalar_tensor_tensor(out=t2, in0=re, scalar=0.0, in1=t2, op0=ALU.is_lt, op1=ALU.mult))
                    elif n == 14:
                        mark(v.tensor_tensor(t1, t1, t2, ALU.add))
                    elif n == 15:
                        mark(v.tensor_scalar(t2, im, 0.0, -2.0, ALU.is_lt, ALU.mult))
                    elif n == 16:
                        v.scalar_tensor_tensor(out=t1, in0=t2, scalar=1.0, in1=t1, op0=ALU.add, op1=ALU.mult).then_inc(pol_v, 1)
                    elif n == 17:
                        dve.wait_ge(pol_a, i * 4 + (3 + SEED))
                        v.tensor_tensor(t0, re, im, ALU.add).then_inc(pol_v, 1)

                def angle(i, n):
                    a, u, w = mo[:, 1, :], z[:, 0, :], z[:, 1, :]
                    linked()
                    if n == 0:
                        dve.wait_ge(mix_ev, i * GROUPS + (GROUPS + SEED))
                        mark(v.tensor_scalar(u, a, 1 / TWO_PI, ROUND, ALU.mult, ALU.add))
                    elif n == 1:
                        mark(v.tensor_scalar(u, u, ROUND, None, ALU.subtract))
                    elif n < 5:
                        mark(v.scalar_tensor_tensor(out=a, in0=u, scalar=-(PI_A, PI_B, PI_C)[n - 2], in1=a, op0=ALU.mult, op1=ALU.add))
                    elif n == 5:
                        mark(v.tensor_scalar(a, a, PI_MAX, -PI_MAX, ALU.min, ALU.max))
                    elif n == 6:
                        mark(v.tensor_scalar(u, a, PI / 2, None, ALU.add))
                    elif n == 7:
                        mark(v.tensor_scalar(w, u, PI, -TWO_PI, ALU.is_gt, ALU.mult))
                    elif n == 8:
                        mark(v.tensor_tensor(u, u, w, ALU.add))
                    elif n == 9:
                        v.tensor_scalar(u, u, PI_MAX, -PI_MAX, ALU.min, ALU.max).then_inc(ang_v, 1)
                    elif n == 10:
                        dve.wait_ge(ang_a, i * 2 + (1 + SEED))
                        mark(v.tensor_tensor(u, u, mo[:, 0, :], ALU.mult))
                    elif n == 11:
                        dve.wait_ge(ang_a, i * 2 + (2 + SEED))
                        v.tensor_tensor(w, a, mo[:, 0, :], ALU.mult).then_inc(ang_v, 1)

                def forward(i, base, late):
                    if not (isinstance(i, int) and i == 0):
                        dve.wait_ge(pol_v, i * 3 + SEED)
                    for c in range(32):
                        dve.wait_ge(pass2, base + (c + 1 + SEED))
                        n, at = (SIDE, c * SIDE) if c < 16 else (HALFW, FRAC + (c - 16) * HALFW)
                        v.tensor_copy(ri[:, :, at:at + n], ps_b[c % 2][:, 0:2 * n].rearrange("p (k n) -> p k n", k=2)).then_inc(taken, 1)
                        if late is not None:
                            if c % 2 == 0 and c // 2 < 10:
                                angle(late, c // 2)
                            if c in (27, 30):
                                angle(late, 10 + (c - 27) // 3)

                def angles(late, early):
                    if late is not None:
                        for n in range(12):
                            angle(late, n)
                    if early is not None:
                        for n in range(18):
                            polar(early, n)
                        close()

                def inverse(i, base, early):
                    if i is None:
                        for n in range(9, 18):
                            polar(early, n)
                        close()
                        return
                    dve.wait_ge(cat_out, i * 16 + 16)
                    for c in range(32):
                        if c < 16:
                            dve.wait_ge(squared, i * 16 + (c + 1 + SEED))
                            ins = v.tensor_tensor(po[:, c, :], sq[c % 2][:, 0:SIDE], sq[c % 2][:, SIDE:256], ALU.add)
                        else:
                            dve.wait_ge(pass2, base + (c + 1 + SEED))
                            ins = v.tensor_copy(po[:, c, :], ps_b[c % 2][:, 0:SIDE])
                        ins.then_inc(taken, 1)
                        if early is not None:
                            if c % 2 == 0 and c // 2 < 8:
                                polar(early, 9 + c // 2)
                            if c == 24:
                                polar(early, 17)
                    dve.wait_ge(taken, base + (32 + SEED))
                    dve.sem_inc(inv_v, 1)
                    close()

                def mixed(i, early):
                    def select(j):
                        dve.wait_ge(mix_ev, i * GROUPS + (17 + j + SEED))
                        dve.sem_inc(closed, 1)
                        s = slice(j * 512, (j + 1) * 512)
                        v.copy_predicated(gm[:, 0, s], msk[:, 1 + 4 * j:5 + 4 * j, :].bitcast(U32).rearrange("p r w -> p (r w)"), gm[:, 1, s]).then_inc(mix_v, 1)

                    def form(*stages):
                        if early is not None:
                            for n in stages:
                                polar(early, n)

                    dve.wait_ge(gm_in, i * 96 + (96 + 16))
                    mark(v.tensor_tensor(mp[:, 1:17, 1:SIDE + 1], gm[:, 0, 0:FRAC].rearrange("p (r w) -> p r w", w=SIDE), msk[:, 1:17, :], ALU.mult))
                    linked()
                    v.tensor_tensor(mp[:, 0:18:17, 1:SIDE + 1], mp[:, 0:18:17, 1:SIDE + 1], msk[:, 0:18:17, :], ALU.mult).then_inc(mix_v, 1)
                    form(0, 1, 2, 3, 4)
                    select(0)
                    form(5, 6)
                    select(1)
                    form(7, 8)
                    select(2)
                    select(3)

                turns(forward, mixed, inverse, angles, dve)


N = SIDE


def fractional_matrix(a):
    alpha = a * np.pi / 2
    tana2, sina = np.tan(alpha / 2), np.sin(alpha)
    up = np.zeros((N, 2 * N - 1))
    up[:, ::2] = np.eye(N)
    sinc = np.sinc(np.arange(-(2 * N - 3), 2 * N - 2) / 2.0)
    fi = np.stack([np.convolve(r, sinc)[2 * N - 3:4 * N - 4] for r in up])
    n = np.arange(-2 * N + 2, 2 * N - 1).astype(np.float64)
    chirp = np.exp(-1j * np.pi / N * tana2 / 4 * n**2)
    pad = np.zeros((N, N - 1))
    fp = np.concatenate([pad, fi, pad], axis=1) * chirp
    c = np.pi / N / sina / 4
    m = np.arange(-(4 * N - 4), 4 * N - 3).astype(np.float64)
    kern = np.exp(1j * c * m**2)
    ret = np.stack([np.convolve(r, kern)[4 * N - 4:8 * N - 7] for r in fp]) * np.sqrt(c / np.pi)
    return (np.exp(-1j * (1 - a) * np.pi / 4) * chirp * ret)[:, N - 1:3 * N - 2:2]


def centered_inverse_matrix():
    shft = (np.arange(N) + N // 2) % N
    return (np.fft.ifft(np.eye(N)[:, shft], axis=-1) * np.sqrt(N))[:, np.argsort(shft)]


def real_pair(m):
    return np.stack([np.concatenate([m.real, m.imag], 1), np.concatenate([-m.imag, m.real], 1)], 1).astype(np.float32)


def shape_constants():
    frac = fractional_matrix(0.5)
    ifrac = centered_inverse_matrix() @ fractional_matrix(0.5)
    k = np.arange(N)
    turn = np.outer(k, k) % N
    cos, sin = np.cos(2 * np.pi * turn / N), np.sin(2 * np.pi * turn / N)
    cos[turn % (N // 2) == N // 4] = 0
    sin[turn % (N // 2) == 0] = 0
    four = cos - 1j * sin
    twice = np.full((HALFW, 1), 2.0)
    twice[0] = twice[-1] = 1
    inv2 = np.stack([twice * cos[:HALFW], -twice * sin[:HALFW]], 1) / N**2
    mask = np.zeros((N + 2, N), np.float32)
    inner = int(N * np.cos(0.5 * np.pi / 2))
    lo = (N - inner) // 2
    mask[lo + 1:lo + 1 + inner, lo:lo + inner] = 1
    mask = np.stack([mask[16 * b:16 * b + 18] for b in range(8) for _ in range(16)])
    return {
        "c_frac": real_pair(frac),
        "c_ifrac": real_pair(ifrac),
        "c_four1": real_pair(four)[:, 0],
        "c_four2": real_pair(four[:, :HALFW]),
        "c_inv1": real_pair(four.conj()),
        "c_inv2": inv2.astype(np.float32),
        "c_mask": mask,
        "c_eye4": np.tile(np.eye(P // 4, dtype=np.float32), (4, 1)),
        "c_sign": np.repeat(np.array([[(-1.0) ** (fy * ry + fx * rx) for ry in range(2) for rx in range(2)] for fy in range(2) for fx in range(2)], np.float32), P // 4, 0),
        "c_gavg": np.kron(np.eye(16), np.full((6, 6), 1 / 6)).astype(np.float32),
    }


def laid_out(w):
    def blocks(m):
        out = np.zeros((P, P), np.float32)
        for b in range(8):
            out[16 * b:16 * b + 16, 16 * b:16 * b + 16] = m.T
        return out

    s = w["L1_conv_mag_s_w"]
    mats = [s[:, :, t // 3, t % 3] for t in range(9)] + [w["L1_conv_mag_f_w"], w["L1_conv_mag_w"], w["L1_conv_pha_w"], w["L1_conv_conv_1_w"]]
    rows = [w["L1_conv_mag_s_b"], w["L1_conv_mag_f_b"], w["L1_conv_mag_b"], w["L1_conv_pha_b"], w["L1_conv_conv_1_b"]]
    dw = w["L0_conv_w_dw"].reshape(-1, 2, 9)
    half = np.zeros((2 * P, 2, 9), np.float32)
    half[:dw.shape[0] // 2] = dw[:dw.shape[0] // 2]
    half = half.reshape(2, 4, P // 4, 2, 9).transpose(2, 1, 0, 3, 4)
    c0 = w["L1_conv_conv_0_w"].shape[0]
    hid = w["L0_conv_w_in"].shape[0]
    w_in = np.zeros((2 * HALF, 2, 2 * P), np.float32)
    for side in range(2):
        w_in[:, side, :hid // 2] = w["L0_conv_w_in"][side * (hid // 2):(side + 1) * (hid // 2), :, 0, 0].T
    return {
        "w_dwA": np.tile(half.reshape(P // 4, 16, 9), (4, 1, 1)),
        "w_in": w_in.reshape(2, HALF, 4, P).transpose(1, 0, 2, 3),
        "w_dw": w["L0_conv_w_dw"].reshape(-1, 9),
        "fft_w": w["L0_conv_fft_w"].reshape(-1, 4),
        "w_outT": w["L0_conv_w_out"][:, :, 0, 0].T,
        "w1T": w["L1_conv_conv1_w"].T,
        "w1x0": w["L1_conv_conv1_w"][:c0].reshape(c0, 2, HALF),
        "w0T": w["L1_conv_conv_0_w"].T,
        "b0": np.concatenate([w["L1_conv_conv_0_b"], np.zeros(2 * c0, np.float32)]).reshape(-1, 1),
        "w2T": np.concatenate([w["L1_conv_conv2_w"].T, np.zeros((HALF - 3 * c0, 2 * HALF), np.float32)]),
        "mixes": np.stack([blocks(m) for m in mats], 1),
        "biases": np.stack([np.tile(r, 8) for r in rows], 1),
    }


def program(nc, d, out, nb):
    y = nc.dram_tensor("y_scratch", [nb, 192, SIDE, SIDE], F32).ap()
    x1 = nc.dram_tensor("x1_scratch", [nb, 48, SIDE, SIDE], F32).ap()
    cat = nc.dram_tensor("cat_scratch", [nb, 48, SIDE, SIDE], F32).ap()
    scratch = [nc.dram_tensor(f"{n}_scratch", [2, 16, SIDE, w], F32).ap() for n, w in (("polar1", SIDE), ("polar2", HALFW), ("back1", SIDE), ("back2", HALFW))]
    with ExitStack() as ctx:
        gavg = ctx.enter_context(nc.sbuf_tensor("gavg", [HALF, HALF], F32))
        agg = ctx.enter_context(nc.sbuf_tensor("agg", [HALF, 2, nb, 2], F32))
        rstd = ctx.enter_context(nc.sbuf_tensor("rstd", [HALF, 2, nb], F32))
        negmr = ctx.enter_context(nc.sbuf_tensor("negmr", [HALF, 2, nb], F32))
        loaded = ctx.enter_context(nc.semaphore("first_loaded"))
        with nc.Block() as block:
            @block.sync
            def _(sp):
                sp.dma_start(gavg[:], d["c_gavg"]).then_inc(loaded, 16)
                sp.wait_ge(loaded, 16)
        norm_stats(nc, d["x"], agg, nb)
        norm_coefficients(nc, "norm0", agg, gavg, rstd, negmr, nb, 1e-5)
        layer0(nc, d["x"], y, d["w_in"], d["w_dw"], d["w_dwA"], d["fft_w"], d["w_outT"], d["c_eye4"], d["c_sign"], agg, rstd, negmr, nb)
        norm_coefficients(nc, "norm1", agg, gavg, rstd, negmr, nb, 1e-5)
        layer1_in(nc, y, d["w1T"], d["w1x0"], d["w0T"], d["b0"], rstd, negmr, x1, cat, nb)
    consts = [d[n] for n in ("c_frac", "c_ifrac", "c_four1", "c_four2", "c_inv1", "c_inv2")]
    layer1_planes(nc, x1, cat, consts, d["mixes"], d["biases"], d["c_mask"], scratch, nb)
    layer1_out(nc, y, cat, d["w2T"], out, nb)


def kernel(**inputs):
    import concourse.bacc as _bacc
    from concourse.bass_utils import run_bass_kernel_spmd as _run

    w = {name: np.asarray(a) for name, a in inputs.items()}
    arrays = {"x": w["x"], **laid_out(w), **shape_constants()}
    arrays = {name: np.ascontiguousarray(a) for name, a in arrays.items()}
    nc = _bacc.Bacc("TRN2", target_bir_lowering=False, num_devices=1)
    d = {name: nc.dram_tensor(name, list(a.shape), F32, kind="ExternalInput").ap() for name, a in arrays.items()}
    out = nc.dram_tensor("out", list(w["x"].shape), F32, kind="ExternalOutput").ap()
    program(nc, d, out, w["x"].shape[0])
    r = _run(nc, [arrays], core_ids=[0])
    return r.results[0]["out"]
```
